# Optimizing a Trainium2 kernel written in Bass

```python
import numpy as np
import jax
import jax.numpy as jnp

def _softmax(x, axis=-1):
    return jax.nn.softmax(x, axis=axis)

def _gelu(x):
    return jax.nn.gelu(x, approximate=True)

def _silu(x):
    return jax.nn.silu(x)

def _sigmoid(x):
    return jax.nn.sigmoid(x)

def _layernorm(x, axis=-1, eps=1e-05):
    m = jnp.mean(x, axis=axis, keepdims=True)
    v = jnp.var(x, axis=axis, keepdims=True)
    return (x - m) / jnp.sqrt(v + eps)

def _scatter_add(tgt, idx, src, axis=0):
    return tgt.at[idx].add(src)

def _segment_sum(src, seg, n):
    return jax.ops.segment_sum(src, seg, n)
kernel_name = 'mk_gnn_resnorm_d2_gnn_r8_799a5f'

def setup_inputs(seed: int=0):
    np.random.seed(seed)
    _w = jnp.asarray

    def _rec_inputs():
        import jax
        import jax.numpy as jnp
        _gk = jax.random.key(seed)
        x = -0.0007083 + 1.001 * jax.random.normal(jax.random.fold_in(_gk, 1), (6250, 48), jnp.float32)
        src = jax.random.randint(jax.random.fold_in(_gk, 2), (200000,), 0, 6250, jnp.int32)
        dst = jnp.minimum((6250 * jax.random.uniform(jax.random.fold_in(_gk, 3), (200000,)) ** 2.0).astype(jnp.int32), 49999)
        _o = jnp.argsort(dst, stable=True)
        src = src[_o]
        dst = dst[_o]
        edge_attr_40 = jax.random.uniform(jax.random.fold_in(_gk, 12), (200000, 40), jnp.float32, 0.0, 1)
        edge_weight = jax.random.uniform(jax.random.fold_in(_gk, 14), (200000,), jnp.float32, 0.0, 7.99999)
        node_type_119 = jax.random.randint(jax.random.fold_in(_gk, 15), (6250,), 0, 119, jnp.int32)
        node_vec = jax.random.uniform(jax.random.fold_in(_gk, 16), (6250,), jnp.float32, 0.0, 3.99996)
        return (x, src, dst, edge_attr_40, edge_weight, node_type_119, node_vec)
    x, src, dst, edge_attr_40, edge_weight, node_type_119, node_vec = _rec_inputs()

    def _L0_gnn_setup():
        import jax, jax.numpy as jnp
        import numpy as np
        N = 6250
        E = 150000
        H = 48
        RBF = 40
        L = 4
        NELEM = 119
        G = 32
        CUT = 6.0

        def _ln(x, g, b):
            m = x.mean(-1, keepdims=True)
            v = ((x - m) ** 2).mean(-1, keepdims=True)
            return (x - m) * jax.lax.rsqrt(v + 1e-05) * g + b
        key = jax.random.key(seed)
        k = jax.random.split(key, 16)
        s = 0.1
        return {'h': jax.random.normal(k[0], (N, H), jnp.float32), 'edge_index': jax.random.randint(k[1], (2, E), 0, N), 'edge_attr': jax.random.uniform(k[2], (E, RBF), dtype=jnp.float32), 'distances': jax.random.uniform(k[3], (E,), dtype=jnp.float32) * 8.0, 'atom_z': jax.random.randint(k[4], (N,), 0, NELEM), 'node_mult': jax.random.uniform(k[5], (N,), dtype=jnp.float32) * 3.0 + 1.0, 'batch': jnp.sort(jax.random.randint(k[6], (N,), 0, 64)), 'Wq': jax.random.normal(k[7], (L, H, H), jnp.float32) * s, 'gq': jnp.ones((L, H), jnp.float32), 'bq': jnp.zeros((L, H), jnp.float32), 'Wk': jax.random.normal(k[8], (L, H, H), jnp.float32) * s, 'gk': jnp.ones((L, H), jnp.float32), 'bk': jnp.zeros((L, H), jnp.float32), 'Wm': jax.random.normal(k[9], (L, H, H), jnp.float32) * s, 'Wu': jax.random.normal(k[10], (L, 2 * H, H), jnp.float32) * s, 'go': jnp.ones((L, H), jnp.float32), 'bo': jnp.zeros((L, H), jnp.float32), 'F1W': jax.random.normal(k[11], (RBF, H), jnp.float32) * s, 'F1b': jnp.zeros((H,), jnp.float32), 'F2W': jax.random.normal(k[12], (H, H), jnp.float32) * s, 'F2b': jnp.zeros((H,), jnp.float32), 'gn': jnp.ones((H,), jnp.float32), 'bn': jnp.zeros((H,), jnp.float32), 'emb': jax.random.normal(k[13], (NELEM, G), jnp.float32) * 0.01, 'adapt': jax.random.normal(k[14], (G, G), jnp.float32) * 0.01}
    _L0_gnn_all = _L0_gnn_setup()
    _L0_gnn_in = {k: v for k, v in _L0_gnn_all.items() if k in ('Wq', 'gq', 'bq', 'Wk', 'gk', 'bk', 'Wm', 'Wu', 'go', 'bo', 'F1W', 'F1b', 'F2W', 'F2b', 'gn', 'bn', 'emb', 'adapt')}
    del _L0_gnn_all

    def _L1_gnn_setup():
        import jax, jax.numpy as jnp
        import numpy as np
        key = jax.random.key(seed)
        k1, k2 = jax.random.split(key)
        N, C, E = (12500, 48, 200000)
        label_mat = jax.random.uniform(k1, (N, C), dtype=jnp.float32)
        edge_index = jax.random.randint(k2, (2, E), 0, N, dtype=jnp.int64)
        return {'label_mat': label_mat, 'edge_index': edge_index, 'num_nodes': N}
    _L1_gnn_all = _L1_gnn_setup()
    _L1_gnn_in = {k: v for k, v in _L1_gnn_all.items() if k in ()}
    del _L1_gnn_all
    return {'x': x, 'src': src, 'dst': dst, 'edge_attr_40': edge_attr_40, 'edge_weight': edge_weight, 'node_type_119': node_type_119, 'node_vec': node_vec, 'L0_gnn_Wq': _L0_gnn_in['Wq'], 'L0_gnn_gq': _L0_gnn_in['gq'], 'L0_gnn_bq': _L0_gnn_in['bq'], 'L0_gnn_Wk': _L0_gnn_in['Wk'], 'L0_gnn_gk': _L0_gnn_in['gk'], 'L0_gnn_bk': _L0_gnn_in['bk'], 'L0_gnn_Wm': _L0_gnn_in['Wm'], 'L0_gnn_Wu': _L0_gnn_in['Wu'], 'L0_gnn_go': _L0_gnn_in['go'], 'L0_gnn_bo': _L0_gnn_in['bo'], 'L0_gnn_F1W': _L0_gnn_in['F1W'], 'L0_gnn_F1b': _L0_gnn_in['F1b'], 'L0_gnn_F2W': _L0_gnn_in['F2W'], 'L0_gnn_F2b': _L0_gnn_in['F2b'], 'L0_gnn_gn': _L0_gnn_in['gn'], 'L0_gnn_bn': _L0_gnn_in['bn'], 'L0_gnn_emb': _L0_gnn_in['emb'], 'L0_gnn_adapt': _L0_gnn_in['adapt']}

def reference(x, src, dst, edge_attr_40, edge_weight, node_type_119, node_vec, L0_gnn_Wq, L0_gnn_gq, L0_gnn_bq, L0_gnn_Wk, L0_gnn_gk, L0_gnn_bk, L0_gnn_Wm, L0_gnn_Wu, L0_gnn_go, L0_gnn_bo, L0_gnn_F1W, L0_gnn_F1b, L0_gnn_F2W, L0_gnn_F2b, L0_gnn_gn, L0_gnn_bn, L0_gnn_emb, L0_gnn_adapt):
    import jax
    import jax.numpy as jnp

    def _L0_gnn_ref(h, edge_index, edge_attr, distances, atom_z, node_mult, batch, Wq, gq, bq, Wk, gk, bk, Wm, Wu, go, bo, F1W, F1b, F2W, F2b, gn, bn, emb, adapt):
        import jax, jax.numpy as jnp
        import numpy as np
        N = 6250
        E = 150000
        H = 48
        RBF = 40
        L = 4
        NELEM = 119
        G = 32
        CUT = 6.0

        def _ln(x, g, b):
            m = x.mean(-1, keepdims=True)
            v = ((x - m) ** 2).mean(-1, keepdims=True)
            return (x - m) * jax.lax.rsqrt(v + 1e-05) * g + b
        src, dst = (edge_index[0], edge_index[1])
        gate = jax.nn.silu(edge_attr @ F1W + F1b) @ F2W + F2b
        ei = emb[atom_z[src]]
        ej = emb[atom_z[dst]]
        gate = gate + (ei * (ej @ adapt)).sum(-1, keepdims=True)
        cw = jnp.where(distances < CUT, 0.5 * (jnp.cos(jnp.pi * distances / CUT) + 1.0), 0.0)
        mj = node_mult[dst]
        msg = gate * h[dst] * (cw * mj)[:, None]
        agg = jax.ops.segment_sum(msg, src, num_segments=N)
        tot = jnp.clip(jax.ops.segment_sum(mj, src, num_segments=N), 1e-08, None)
        h = _ln(h + agg / tot[:, None], gn, bn)
        logm = jnp.log(jnp.clip(node_mult, 1.0, None))
        for i in range(L):
            Q = _ln(h @ Wq[i], gq[i], bq[i])
            K = _ln(h @ Wk[i], gk[i], bk[i])
            qi = Q[src]
            kj = K[dst]
            score = (qi * kj).sum(-1) + 0.1 * (edge_attr * qi[:, :RBF]).sum(-1) + logm[dst]
            smax = jax.ops.segment_max(score, src, num_segments=N)
            es = jnp.exp(jnp.minimum(score - smax[src], 20.0))
            denom = jax.ops.segment_sum(es, src, num_segments=N)
            alpha = es / (denom[src] + 1e-10)
            m = h[dst] @ Wm[i]
            aggi = jax.ops.segment_sum(alpha[:, None] * m, src, num_segments=N)
            z = jnp.concatenate([h, aggi], axis=-1) @ Wu[i]
            z = jnp.where(z > 0, z, 0.01 * z)
            h = _ln(h + z, go[i], bo[i])
        return h

    def _L1_gnn_ref(label_mat, edge_index, num_nodes):
        import jax, jax.numpy as jnp
        import numpy as np
        row, col = (edge_index[0], edge_index[1])
        self_loop = jnp.arange(num_nodes, dtype=row.dtype)
        row = jnp.concatenate([row, self_loop])
        col = jnp.concatenate([col, self_loop])
        ones = jnp.ones_like(row, dtype=label_mat.dtype)
        deg = jax.ops.segment_sum(ones, row, num_segments=num_nodes)
        deg_inv_sqrt = jnp.where(deg > 0, jax.lax.rsqrt(deg), 0.0)
        norm = deg_inv_sqrt[row] * deg_inv_sqrt[col]
        msgs = label_mat[row] * norm[:, None]
        out = jax.ops.segment_sum(msgs, col, num_segments=num_nodes)
        return out
    edge_index = jnp.stack([src, dst])
    batch0 = jnp.zeros((6250,), jnp.int32)
    x = _layernorm(x + _L0_gnn_ref(x, edge_index, edge_attr_40, edge_weight, node_type_119, node_vec, batch0, L0_gnn_Wq, L0_gnn_gq, L0_gnn_bq, L0_gnn_Wk, L0_gnn_gk, L0_gnn_bk, L0_gnn_Wm, L0_gnn_Wu, L0_gnn_go, L0_gnn_bo, L0_gnn_F1W, L0_gnn_F1b, L0_gnn_F2W, L0_gnn_F2b, L0_gnn_gn, L0_gnn_bn, L0_gnn_emb, L0_gnn_adapt), axis=-1)
    x = _layernorm(x + _L1_gnn_ref(x, edge_index, 6250), axis=-1)
    return x

_drawn_inputs = setup_inputs


def setup_inputs(seed=0):
    import zlib

    import numpy as np

    out = dict(_drawn_inputs(seed))
    spreads = {'L0_gnn_gq': (1.0, 0.2),
     'L0_gnn_bq': (0.0, 0.1),
     'L0_gnn_gk': (1.0, 0.2),
     'L0_gnn_bk': (0.0, 2.0),
     'L0_gnn_go': (1.0, 0.2),
     'L0_gnn_bo': (0.0, 0.1),
     'L0_gnn_F1b': (0.0, 2.0),
     'L0_gnn_F2b': (0.0, 0.468),
     'L0_gnn_gn': (1.0, 0.2),
     'L0_gnn_bn': (0.0, 0.1)}
    factors = {'L0_gnn_emb': 64.0, 'L0_gnn_adapt': 64.0}
    for name, (base, spread) in spreads.items():
        noise = np.random.default_rng([zlib.crc32(name.encode()), seed]).standard_normal(out[name].shape)
        drawn = base * np.exp(spread * noise) if base else spread * noise
        out[name] = jnp.asarray(drawn.astype(out[name].dtype))
    for name, factor in factors.items():
        out[name] = (out[name] * factor).astype(out[name].dtype)
    return out
```

```python
from contextlib import ExitStack

import concourse.bass as bass
from concourse import mybir

F32 = mybir.dt.float32
I32 = mybir.dt.int32
BF16 = mybir.dt.bfloat16
ALU = mybir.AluOpType
ACT = mybir.ActivationFunctionType
AX = mybir.AxisListType.X

P = 128
N = 6250
E = 200000
H = 48
RBF = 40
L = 4
GF = 32
NELEM = 119
NB = (N + P) // P
NN = NB * P
T = 1568
S = P * T
TC = 28
PAIRS = T // TC // 2
ROW = 44
C_CW, C_DST, C_SRC = 40, 41, 42
ST = 50
ZROW = S + P
RT = 8
RPAIRS = T // RT // 2
RQ = 4
RLOOPS = T // RT // RQ
HC = 112
OFF = 64
BIG = 1e30
CUT = 6.0
PI = 3.14159265358979


class Chain:

    def __init__(self, eng, sem, base=0):
        self.eng, self.sem, self.base, self.k = eng, sem, base, 0

    def link(self, ins):
        self.k += 1
        ins.then_inc(self.sem, 1)
        self.eng.wait_ge(self.sem, self.base + self.k)

    def end(self, ins):
        self.k += 1
        ins.then_inc(self.sem, 1)

    def last(self, per):
        assert self.k == per, (self.k, per)


def flat(ap):
    return ap.rearrange("p a b -> p (a b)")


def build(nc, a):
    root = ExitStack()
    with root:
        def sb(name, shape, dt=F32, ctx=root):
            return ctx.enter_context(nc.sbuf_tensor(name, shape, dt))

        def sem(name, ctx=root):
            return ctx.enter_context(nc.semaphore(name))

        def cleared(sems):
            with nc.Block() as block:
                @block.gpsimd
                def _(pool):
                    for s in sems:
                        nc.gpsimd.sem_clear(s)

        def two(name, ctx=root):
            return [sem(f"{name}{h}", ctx) for h in range(2)]

        bank = [root.enter_context(nc.psum_tensor(f"bank{i}", [P, 512], F32)) for i in range(8)]

        edges = nc.dram_tensor("edges_by_src", (S, ROW), F32, kind="Internal").ap()
        bydst = nc.dram_tensor("edges_by_dst", (S, 2), I32, kind="Internal").ap()
        fill = nc.dram_tensor("fill_rows", (S + NN, H), F32, kind="Internal").ap()
        state = nc.dram_tensor("state_rows", (S + P + 1, ST), F32, kind="Internal").ap()
        nodes = nc.dram_tensor("node_rows", (NN, 2 * H), F32, kind="Internal").ap()
        elems = nc.dram_tensor("element_rows", (NELEM, 2 * GF), F32, kind="Internal").ap()

        iota_f = sb("iota_f", [P, P])
        pidx = sb("pidx", [P, 1])
        ident = sb("ident", [P, P])
        ident_b = sb("ident_b", [P, P], BF16)
        before = sb("before", [P, P])
        after = sb("after", [P, P])
        ones = sb("ones", [P, P])
        iota_b = sb("iota_b", [P, P], BF16)
        count = [sb(f"count{k}", [P, NB]) for k in range(2)]
        first_i = sb("first_i", [P, NB], I32)
        last_i = [sb(f"last_i{k}", [P, NB], I32) for k in range(2)]

        zero_dma = sem("zero_dma")
        const_ready = sem("const_ready")
        const_chain = sem("const_chain")
        iota_done = sem("iota_done")

        with ExitStack() as ctx:
            iota_i = sb("iota_i", [P, P], I32, ctx)
            pidx_i = sb("pidx_i", [P, 1], I32, ctx)
            zeros = sb("zeros", [P, TC * H], F32, ctx)
            block = ctx.enter_context(nc.Block())

            @block.gpsimd
            def _(pool):
                nc.gpsimd.iota(iota_i[:, :], [[1, P]], base=0, channel_multiplier=0).then_inc(iota_done, 1)
                nc.gpsimd.iota(pidx_i[:, :], [[0, 1]], base=0, channel_multiplier=1).then_inc(iota_done, 1)

            @block.vector
            def _(dve):
                c = Chain(dve, const_chain)
                nc.vector.memset(zeros[:, :], 0.0).then_inc(const_ready, 1)
                dve.wait_ge(iota_done, 2)
                c.link(nc.vector.tensor_copy(iota_f[:, :], iota_i[:, :]))
                c.link(nc.vector.tensor_copy(pidx[:, :], pidx_i[:, :]))
                c.link(nc.vector.tensor_copy(iota_b[:, :], iota_f[:, :]))
                c.link(nc.vector.memset(ones[:, :], 1.0))
                for out, op in ((ident, ALU.is_equal), (ident_b, ALU.is_equal), (before, ALU.is_lt),
                                (after, ALU.is_gt)):
                    c.link(nc.vector.tensor_scalar(out[:, :], iota_f[:, :], pidx[:, 0:1], None, op))

            @block.sync
            def _(sp):
                sp.wait_ge(const_ready, 1)
                fill_v = fill[0:S, :].rearrange("(p t) f -> p (t f)", p=P)
                with sp.Fori(0, T // TC) as i:
                    sp.dma_start(fill_v[:, bass.ds(i * (TC * H), TC * H)], zeros[:, :]).then_inc(zero_dma, 16)
                sp.dma_start(state[S:S + P, :], zeros[:, 0:ST]).then_inc(zero_dma, 16)
                sp.dma_start(state[ZROW:ZROW + 1, :], zeros[0:1, 0:ST]).then_inc(zero_dma, 16)
                sp.wait_ge(zero_dma, 16 * (T // TC + 2))

        def sort(key):
            tag = "sd"[key]
            keys_in = a["dst_cols" if key else "src_cols"]
            other_in = a["src_cols" if key else "dst_cols"]
            with ExitStack() as sems_ctx, ExitStack() as clear_ctx, ExitStack() as ctx:
                def s_(name, shape, dt=F32):
                    return sb(f"{name}_{tag}", shape, dt, ctx)

                used = []

                def m_(name):
                    used.append(sem(f"{name}_{tag}", sems_ctx))
                    return used[-1]

                def mm_(name, k=2):
                    return [m_(f"{name}{h}") for h in range(k)]

                key_i = s_("key_i", [P, T], I32)
                oth_i = s_("oth_i", [P, T], I32)
                key_f = s_("key_f", [P, T])
                part_i = s_("part_i", [P, T], I32)
                lo_b = s_("lo_b", [P, T + RT], BF16)
                hi_b = s_("hi_b", [P, T + RT], BF16)
                w_all = s_("w_all", [P, T])
                w_tmp = s_("w_tmp", [P, T])
                half_pi = s_("half_pi", [P, 1])
                lo1 = [s_(f"lo1_{h}", [P, RT, P], BF16) for h in range(2)]
                hi1 = [s_(f"hi1_{h}", [P, RT, NB], BF16) for h in range(2)]
                lo1T = [s_(f"lo1T_{h}", [P, RT * P]) for h in range(2)]
                keyrow = [s_(f"keyrow_{h}", [P, RT * P], I32) for h in range(2)]
                seen = s_("seen", [P, RT + 1, NB])
                prod = s_("prod", [P, RT, NB])
                junk = s_("junk", [P, P])
                within = s_("within", [P, RT])
                base = s_("base", [P, RT])
                pos = [s_(f"pos_{q}", [P, RT], I32) for q in range(RQ)]
                rows = [s_(f"rows_{q}", [P, RT, ROW if key == 0 else 2], F32 if key == 0 else I32)
                        for q in range(RQ)]
                tot = s_("tot", [P, NB])
                incl = s_("incl", [P, NB])
                tmp = s_("tmp", [P, NB])
                mask = s_("mask", [P, NB])
                if key == 1:
                    pairs = s_("pairs", [P, T, 2], I32)
                    falls = s_("falls", [P, 1])
                    unsorted_i = s_("unsorted_i", [P, 1], I32)

                clear_ctx.callback(cleared, used)
                loaded, prep, chain = m_("loaded"), m_("prep"), m_("chain")
                hist_in, hist_out = mm_("hist_in"), m_("hist_out")
                hot, hist, prefix = mm_("hot"), mm_("tile_counts"), m_("prefix")
                seen_ok, got = mm_("seen_ok"), mm_("got")
                turned, turned_sb = mm_("turned"), mm_("turned_sb")
                row_dma, key_dma = mm_("row_dma", RQ), mm_("key_dma")
                sent = [sem(f"sent_{tag}{q}") for q in range(RQ)]
                keys_used, pos_ok = mm_("keys_used"), mm_("pos_ok", RQ)
                payload, rows_free = mm_("payload", RQ), mm_("rows_free", RQ)
                go, rank_chain = m_("go"), m_("rank_chain")
                sine, wchain = m_("sine"), m_("wchain")
                next_in, paired, falls_in = m_("next_in"), m_("paired"), m_("falls_in")
                pairs_out = m_("pairs_out")
                tile_counts = [bank[0], bank[1]]
                got_ps = [bank[2], bank[3]]
                turn_ps = [bank[4], bank[5]]
                hist_ps = bank[6]
                tot_ps = bank[7]
                ea_v = a["edge_attr"].rearrange("(p t) f -> p t f", p=P)

                def one_hot(h, c0):
                    nc.vector.tensor_tensor(
                        lo1[h][:, :, :], iota_b[:, :].unsqueeze(1).broadcast_to([P, RT, P]),
                        lo_b[:, bass.ds(c0, RT)].unsqueeze(2).broadcast_to([P, RT, P]), ALU.is_equal)
                    nc.vector.tensor_tensor(
                        hi1[h][:, :, :], iota_b[:, 0:NB].unsqueeze(1).broadcast_to([P, RT, NB]),
                        hi_b[:, bass.ds(c0, RT)].unsqueeze(2).broadcast_to([P, RT, NB]), ALU.is_equal
                    ).then_inc(hist_in[h], 1)

                with nc.Block() as block:
                    @block.sync
                    def _(sp):
                        sp.dma_start(key_i[:, :], keys_in[:, :]).then_inc(loaded, 16)
                        sp.dma_start(oth_i[:, :], other_in[:, :]).then_inc(loaded, 16)
                        sp.dma_start(w_tmp[:, :], a["edge_weight"][:, :]).then_inc(loaded, 16)
                        if key == 1:
                            line = keys_in.rearrange("p t -> (p t)")
                            last_row = (P - 1) * T
                            sp.wait_ge(prep, 1)
                            sp.dma_start(part_i[0:P - 1, :],
                                         line[1:1 + last_row].rearrange("(p t) -> p t", t=T)).then_inc(next_in, 16)
                            sp.dma_start(part_i[P - 1:P, 0:T - 1],
                                         line[1 + last_row:S].rearrange("(p t) -> p t", p=1)).then_inc(next_in, 16)
                            sp.wait_ge(paired, 1)
                            sp.dma_start(bydst.rearrange("(p t) f -> p t f", p=P), pairs[:, :, :]
                                         ).then_inc(pairs_out, 16)
                            sp.wait_ge(pairs_out, 16)

                    @block.scalar
                    def _(act):
                        if key == 0:
                            act.wait_ge(wchain, 9)
                            nc.scalar.activation(w_all[:, :], w_all[:, :], ACT.Sin, bias=half_pi[:, 0:1],
                                                 scale=-PI / CUT).then_inc(sine, 1)
                        else:
                            act.wait_ge(loaded, 48)
                            nc.scalar.copy(pairs[:, :, 0], oth_i[:, :])
                            nc.scalar.copy(pairs[:, :, 1], key_i[:, :]).then_inc(paired, 1)

                    @block.tensor
                    def _(pe):
                        pe.wait_ge(prep, 1)
                        nc.tensor.matmul(hist_ps[:, 0:NB], lo1[0][:, 0, :], hi1[0][:, 0, :], start=True, stop=False,
                                         skip_group_check=True).then_inc(hist_out, 1)
                        if key == 1:
                            pe.wait_ge(falls_in, 1)
                            nc.tensor.matmul(tile_counts[0][:, 0:1], ones[:, :], falls[:, :], start=True, stop=True
                                             ).then_inc(falls_in, 1)
                        with pe.Fori(0, RPAIRS) as i:
                            for h in range(2):
                                pe.wait_ge(hist_in[h], i + 1)
                                for j in range(RT):
                                    ins = nc.tensor.matmul(hist_ps[:, 0:NB], lo1[h][:, j, :], hi1[h][:, j, :],
                                                           start=False, stop=False, skip_group_check=True)
                                ins.then_inc(hot[h], 1)
                        pe.wait_ge(prep, 2)
                        nc.tensor.matmul(hist_ps[:, 0:NB], lo1[0][:, 0, :], hi1[0][:, 0, :], start=False, stop=True,
                                         skip_group_check=True).then_inc(hist_out, 1)
                        pe.wait_ge(prep, 3)
                        nc.tensor.matmul(tot_ps[:, 0:NB], ones[:, :], count[key][:, :], start=True, stop=True)
                        nc.tensor.matmul(tot_ps[:, 64:64 + NB], after[:, :], count[key][:, :], start=True,
                                         stop=True).then_inc(prefix, 1)

                    @block.vector
                    def _(dve):
                        c = Chain(dve, chain)
                        w = Chain(dve, wchain)
                        c.link(nc.vector.memset(half_pi[:, :], PI / 2))
                        c.link(nc.vector.memset(lo_b[:, T:T + RT], 0.0))
                        c.link(nc.vector.memset(hi_b[:, T:T + RT], 0.0))
                        c.link(nc.vector.memset(lo1[0][:, 0, :], 0.0))
                        if key == 1:
                            c.link(nc.vector.memset(part_i[:, :], NN))
                        nc.vector.memset(hi1[0][:, 0, :], 0.0).then_inc(prep, 1)
                        dve.wait_ge(prep, 1)
                        dve.wait_ge(loaded, 48)
                        if key == 0:
                            w.link(nc.vector.tensor_single_scalar(w_all[:, :], w_tmp[:, :], 0.5 / CUT, ALU.mult))
                            w.link(nc.vector.tensor_copy(part_i[:, :], w_all[:, :]))
                            w.link(nc.vector.tensor_copy(w_all[:, :], part_i[:, :]))
                            w.link(nc.vector.scalar_tensor_tensor(w_all[:, :], w_all[:, :], -2 * CUT, w_tmp[:, :],
                                                                  ALU.mult, ALU.add))
                            w.link(nc.vector.scalar_tensor_tensor(w_all[:, :], w_all[:, :], -1.0, w_all[:, :],
                                                                  ALU.mult, ALU.max))
                            w.link(nc.vector.tensor_scalar(key_f[:, :], w_all[:, :], -1.0, 2 * CUT, ALU.mult, ALU.add))
                            w.link(nc.vector.tensor_tensor(w_all[:, :], w_all[:, :], key_f[:, :], ALU.min))
                            w.link(nc.vector.tensor_scalar(w_tmp[:, :], w_tmp[:, :], CUT, None, ALU.is_lt))
                            w.link(nc.vector.tensor_scalar(w_all[:, :], w_all[:, :], 0.0, None, ALU.max))
                        else:
                            dve.wait_ge(next_in, 32)
                            c.link(nc.vector.tensor_tensor(w_all[:, :], part_i[:, :], key_i[:, :], ALU.is_lt))
                            nc.vector.tensor_reduce(falls[:, :], w_all[:, :], AX, ALU.add).then_inc(falls_in, 1)
                            dve.wait_ge(falls_in, 2)
                            c.link(nc.vector.tensor_copy(unsorted_i[:, :], tile_counts[0][:, 0:1]))
                        c.link(nc.vector.tensor_copy(key_f[:, :], key_i[:, :]))
                        c.link(nc.vector.tensor_single_scalar(part_i[:, :], key_i[:, :], P - 1, ALU.bitwise_and))
                        c.link(nc.vector.tensor_copy(lo_b[:, 0:T], part_i[:, :]))
                        c.link(nc.vector.tensor_single_scalar(part_i[:, :], key_i[:, :], 7, ALU.logical_shift_right))
                        c.link(nc.vector.tensor_copy(hi_b[:, 0:T], part_i[:, :]))
                        dve.wait_ge(hist_out, 1)
                        for h in range(2):
                            nc.vector.sem_inc(hot[h], 1)
                        with dve.Fori(0, RPAIRS) as i:
                            for h in range(2):
                                dve.wait_ge(hot[h], i + 1)
                                one_hot(h, (2 * i + h) * RT)
                        if key == 0:
                            dve.wait_ge(sine, 1)
                            w.link(nc.vector.tensor_scalar(w_all[:, :], w_all[:, :], 0.5, 0.5, ALU.mult, ALU.add))
                            w.link(nc.vector.tensor_tensor(w_all[:, :], w_all[:, :], w_tmp[:, :], ALU.mult))
                        for h in range(2):
                            dve.wait_ge(hot[h], RPAIRS + 1)
                        c.link(nc.vector.memset(lo1[0][:, 0, :], 0.0))
                        nc.vector.memset(hi1[0][:, 0, :], 0.0).then_inc(prep, 1)
                        dve.wait_ge(hist_out, 2)
                        nc.vector.tensor_copy(count[key][:, :], hist_ps[:, 0:NB]).then_inc(prep, 1)
                        dve.wait_ge(prep, 3)
                        dve.wait_ge(prefix, 1)
                        c.link(nc.vector.tensor_copy(tot[:, :], tot_ps[:, 0:NB]))
                        c.link(nc.vector.tensor_tensor_scan(incl[:, :], ones[:, 0:NB], tot[:, :], 0.0,
                                                            ALU.mult, ALU.add))
                        c.link(nc.vector.tensor_tensor(incl[:, :], incl[:, :], tot[:, :], ALU.subtract))
                        c.link(nc.vector.tensor_tensor(seen[:, RT, :], incl[:, :], tot_ps[:, 64:64 + NB], ALU.add))
                        c.link(nc.vector.tensor_single_scalar(mask[:, :], count[key][:, :], 0.0, ALU.is_gt))
                        c.link(nc.vector.tensor_tensor(tmp[:, :], seen[:, RT, :], count[key][:, :], ALU.add))
                        c.link(nc.vector.tensor_single_scalar(tmp[:, :], tmp[:, :], -1.0 - ZROW, ALU.add))
                        c.link(nc.vector.tensor_tensor(tmp[:, :], tmp[:, :], mask[:, :], ALU.mult))
                        c.link(nc.vector.tensor_single_scalar(tmp[:, :], tmp[:, :], float(ZROW), ALU.add))
                        c.link(nc.vector.tensor_copy(last_i[key][:, :], tmp[:, :]))
                        if key == 0:
                            c.link(nc.vector.tensor_scalar(incl[:, :], iota_f[:, 0:NB], float(P), pidx[:, 0:1],
                                                           ALU.mult, ALU.add))
                            c.link(nc.vector.tensor_single_scalar(incl[:, :], incl[:, :], float(S), ALU.add))
                            c.link(nc.vector.tensor_tensor(tmp[:, :], seen[:, RT, :], incl[:, :], ALU.subtract))
                            c.link(nc.vector.tensor_tensor(tmp[:, :], tmp[:, :], mask[:, :], ALU.mult))
                            c.link(nc.vector.tensor_tensor(tmp[:, :], tmp[:, :], incl[:, :], ALU.add))
                            c.link(nc.vector.tensor_copy(first_i[:, :], tmp[:, :]))

                def rank():
                    with nc.Block() as block:
                        rank_block(block)

                def rank_block(block):
                    @block.sync
                    def _(sp):
                        krow = a["dst_rows" if key else "src_rows"]

                        def load(i, q):
                            k = RQ * i + q
                            sp.dma_start(keyrow[q % 2][:, :],
                                         krow[:, bass.ds(k * (RT * P), RT * P)].broadcast_to([P, RT * P])
                                         ).then_inc(key_dma[q % 2], 16)
                            if key == 0:
                                sp.dma_start(rows[q][:, :, 0:RBF], ea_v[:, bass.ds(k * RT, RT), :]
                                             ).then_inc(row_dma[q], 16)

                        for q in range(RQ):
                            nc.sync.sem_inc(rows_free[q], 1)
                            if q >= 2:
                                sp.wait_ge(keys_used[q % 2], q // 2)
                            load(0, q)
                        with sp.Fori(1, RLOOPS) as i:
                            for q in range(RQ):
                                sp.wait_ge(sent[q], 16 * RT * i)
                                nc.sync.sem_inc(rows_free[q], 1)
                                sp.wait_ge(keys_used[q % 2], (RQ // 2) * i + q // 2)
                                load(i, q)
                        for q in range(RQ):
                            sp.wait_ge(sent[q], 16 * RT * RLOOPS)

                    @block.scalar
                    def _(act):
                        with act.Fori(0, RLOOPS) as i:
                            for q in range(RQ):
                                h, n = q % 2, (RQ // 2) * i + q // 2 + 1
                                c0 = (RQ * i + q) * RT
                                act.wait_ge(turned[h], n)
                                nc.scalar.copy(lo1T[h][:, :], bank_bf(turn_ps[h])).then_inc(turned_sb[h], 1)
                                act.wait_ge(rows_free[q], i + 1)
                                if key == 0:
                                    act.wait_ge(row_dma[q], 16 * i + 16)
                                    nc.scalar.copy(rows[q][:, :, C_CW], w_all[:, bass.ds(c0, RT)])
                                    nc.scalar.copy(rows[q][:, :, C_DST].bitcast(I32), oth_i[:, bass.ds(c0, RT)])
                                    nc.scalar.copy(rows[q][:, :, C_SRC + 1], key_f[:, bass.ds(c0, RT)])
                                    nc.scalar.copy(rows[q][:, :, C_SRC].bitcast(I32),
                                                   key_i[:, bass.ds(c0, RT)]).then_inc(payload[q], 1)
                                else:
                                    nc.scalar.copy(rows[q][:, :, 0], oth_i[:, bass.ds(c0, RT)])
                                    nc.scalar.copy(rows[q][:, :, 1], key_i[:, bass.ds(c0, RT)]
                                                   ).then_inc(payload[q], 1)

                    @block.gpsimd
                    def _(pool):
                        out = edges if key == 0 else bydst
                        with pool.Fori(0, RLOOPS) as i:
                            for q in range(RQ):
                                pool.wait_ge(pos_ok[q], i + 1)
                                pool.wait_ge(payload[q], i + 1)
                                nc.gpsimd.sem_inc(go, 1)
                                for j in range(RT):
                                    nc.gpsimd.indirect_dma_start(
                                        out=out[:, :],
                                        out_offset=bass.IndirectOffsetOnAxis(ap=pos[q][:, j:j + 1], axis=0),
                                        in_=rows[q][:, j, :], in_offset=None).then_inc(sent[q], 16)

                    @block.tensor
                    def _(pe):
                        with pe.Fori(0, RLOOPS) as i:
                            for q in range(RQ):
                                h, n = q % 2, (RQ // 2) * i + q // 2 + 1
                                pe.wait_ge(hist_in[h], RPAIRS + n)
                                for j in range(RT):
                                    nc.tensor.transpose(bank_bf(turn_ps[h])[:, j * P:(j + 1) * P], lo1[h][:, j, :],
                                                        ident_b[:, :])
                                nc.tensor.matmul(tile_counts[h][:, 0:NB], lo1[h][:, 0, :], hi1[h][:, 0, :],
                                                 start=True, stop=True).then_inc(turned[h], 1)
                                for j in range(1, RT):
                                    ins = nc.tensor.matmul(tile_counts[h][:, j * NB:(j + 1) * NB], lo1[h][:, j, :],
                                                           hi1[h][:, j, :], start=True, stop=True)
                                ins.then_inc(hist[h], 1)
                                pe.wait_ge(turned_sb[h], n)
                                pe.wait_ge(seen_ok[h], n)
                                for j in range(RT):
                                    ins = nc.tensor.matmul(got_ps[h][:, j * NB:(j + 1) * NB],
                                                           lo1T[h][:, j * P:(j + 1) * P], seen[:, j, :],
                                                           start=True, stop=True)
                                ins.then_inc(got[h], 1)

                    @block.vector
                    def _(dve):
                        one_hot(0, 0)
                        per = RQ * (1 + 2 * (RT - 1) + 3)
                        with dve.Fori(0, RLOOPS) as i:
                            c = Chain(dve, rank_chain, per * i)
                            for q in range(RQ):
                                h, n = q % 2, (RQ // 2) * i + q // 2 + 1
                                k = RQ * i + q
                                dve.wait_ge(hist[h], n)
                                dve.wait_ge(key_dma[h], 16 * n)
                                c.link(nc.vector.tensor_copy(seen[:, 0, :], seen[:, RT, :]))
                                for j in range(RT):
                                    add = nc.vector.tensor_tensor(seen[:, j + 1, :], seen[:, j, :],
                                                                  tile_counts[h][:, j * NB:(j + 1) * NB], ALU.add)
                                    add.then_inc(seen_ok[h] if j == RT - 1 else rank_chain, 1)
                                    nc.vector.scalar_tensor_tensor(
                                        junk[:, :], keyrow[h][:, j * P:(j + 1) * P],
                                        key_f[:, bass.ds(k * RT + j, 1)],
                                        before[:, :], ALU.is_equal, ALU.mult, accum_out=within[:, j:j + 1]
                                    ).then_inc(keys_used[h] if j == RT - 1 else rank_chain, 1)
                                    if j == RT - 1:
                                        dve.wait_ge(seen_ok[h], n)
                                        dve.wait_ge(keys_used[h], n)
                                    else:
                                        c.k += 2
                                        dve.wait_ge(rank_chain, c.base + c.k)
                                one_hot(1 - h, (k + 1) * RT)
                                dve.wait_ge(got[h], n)
                                c.link(nc.vector.tensor_tensor(
                                    prod[:, :, :], got_ps[h][:, 0:RT * NB].rearrange("p (j n) -> p j n", j=RT),
                                    hi1[h][:, :, :], ALU.mult))
                                c.link(nc.vector.tensor_reduce(base[:, :], prod[:, :, :], AX, ALU.add))
                                c.link(nc.vector.tensor_tensor(base[:, :], base[:, :], within[:, :], ALU.add))
                                dve.wait_ge(rows_free[q], i + 1)
                                nc.vector.tensor_copy(pos[q][:, :], base[:, :]).then_inc(pos_ok[q], 1)
                            c.last(per)

                if key == 0:
                    rank()
                else:
                    with nc.If(nc.values_load(unsorted_i[0:1, 0:1], min_val=0, max_val=S) > 0):
                        rank()

        def bank_bf(b):
            return b[:, :].bitcast(BF16)

        sort(0)
        sort(1)
        passes(nc, a, root, sb, sem, two, bank, (edges, bydst, fill, state, nodes, elems),
               (iota_f, pidx, ident, ones, count, first_i, last_i))


NGRP = (NB + 3) // 4
GATE_BANK = 10


def pass_sems(two, sem):
    names = ("row_landed", "fill_landed", "so_stored", "rows_used", "g_used", "qi_ready",
             "prod_done", "s_ready", "coef_ready", "v_done", "so_ready", "flags_ready", "cf_ready")
    d = {n: two(n) for n in names}
    for kind in ("init", "layer", "nbr"):
        d["g_landed", kind] = two(f"g_landed_{kind}")
        d["chain", kind] = sem(f"pass_chain_{kind}")
    return d


def passes(nc, a, root, sb, sem, two, bank, tabs, cst):
    edges, bydst, fill, state, nodes, elems = tabs
    iota_f, pidx, ident, ones, count, first_i, last_i = cst
    qnodes = nc.dram_tensor("source_rows", (NN, H), F32, kind="Internal").ap()
    NCH = T // TC

    srcf = sb("srcf", [P, T])
    same = sb("same", [P, T])
    logm = sb("logm", [P, T])
    hc = sb("hc", [P, NB, HC])
    g_all = sb("g_all", [P, 2, TC, 2 * H])
    pf_all = sb("pf_all", [P, 4, TC * H])
    x2 = g_all[:, :, :, :].rearrange("p a t f -> p (a t f)")
    sq_all = pf_all[:, :, :].rearrange("p a f -> p (a f)")
    ns = sb("ns", [P, NB, ST])
    ea = [sb(f"ea{h}", [P, TC, ROW]) for h in range(2)]
    pair_i = [sb(f"pair_i{h}", [P, TC, 2], I32) for h in range(2)]
    qi = [sb(f"qi{h}", [P, H, TC + 1]) for h in range(2)]
    cf = [sb(f"cf{h}", [P, H + 1, TC + 1]) for h in range(2)]
    ce = [sb(f"ce{h}", [P, H + 1, TC + 1]) for h in range(2)]
    v = [sb(f"v{h}", [P, H + 1, TC + 1]) for h in range(2)]
    so = [sb(f"so{h}", [P, TC, ST]) for h in range(2)]
    sc = [sb(f"sc{h}", [P, TC]) for h in range(2)]
    mx = [sb(f"mx{h}", [P, TC + 1]) for h in range(2)]
    k1 = [sb(f"k1{h}", [P, TC + 1]) for h in range(2)]
    d1 = [sb(f"d1{h}", [P, TC]) for h in range(2)]
    d2 = [sb(f"d2{h}", [P, TC]) for h in range(2)]
    es = [sb(f"es{h}", [P, TC]) for h in range(2)]
    pen = sb("pen", [P, TC])
    qc = sb("qc", [P, H])
    vc = sb("vc", [P, H + 1])
    mc = sb("mc", [P, 1])
    kc = sb("kc", [P, 1])
    q0 = sb("q0", [P, H])
    first_key = sb("first_key", [P, 1], I32)
    prevf = sb("prevf", [P, 1])
    lastf = sb("lastf", [P, 1])
    cont = sb("cont", [P, 1])
    nrun = sb("nrun", [P, 1])
    fix_f = sb("fix_f", [P, 1])
    fix_i = sb("fix_i", [P, 1], I32)
    diag = sb("diag", [P, P])
    chb = sb("chb", [H + 1, P])
    penc = sb("penc", [H + 1, P])
    mr = sb("mr", [H + 1, P])
    mcar = sb("mcar", [H + 1, P + 1])
    arg = sb("arg", [H + 1, 2 * P])
    vcar = sb("vcar", [H + 1, P + 1])
    fx = sb("fx", [P, ST])
    fm = sb("fm", [P, 1])
    fa = sb("fa", [P, 2])
    stat = sb("stat", [P, 2 * NB])
    htg = [sb(f"htg{h}", [HC, 4 * P]) for h in range(2)]
    wqk = sb("wqk", [H, 2 * H])
    wu = sb("wu", [HC, H])
    wub = sb("wub", [H, H])
    wmT = sb("wmT", [H, H])
    gb = sb("gb", [P, 6, H])
    gn = sb("gn", [P, 2, H])
    f1w = sb("f1w", [RBF, H])
    f1b = sb("f1b", [H, 1])
    f2 = sb("f2", [H + 1, H])
    eaT = [sb(f"eaT{h}", [RBF, 4 * P]) for h in range(2)]
    hid = sb("hid", [64, 4 * P])
    dis = sb("dis", [P, NB])

    PS = pass_sems(two, sem)
    xv96 = x2[:, 0:NB * 2 * H].rearrange("p (n f) -> p n f", f=2 * H)
    xv48 = x2[:, 0:NB * H].rearrange("p (n f) -> p n f", f=H)
    sem_rows = sem("setup_dma")
    setup_chain = sem("setup_chain")
    emb_ps = sem("emb_ps")
    emb_sb = sem("emb_sb")
    ee_dma = sem("ee_dma")
    ee_rows = sem("ee_rows")
    go, pe_go = sem("pool_go"), sem("pe_go")

    def root_site(name):
        return sem(f"var_{name}"), sem(f"std_{name}")

    def take_root(act, site, run, n):
        act.wait_ge(site[0], run + 1)
        nc.scalar.activation(stat[:, 0:n], stat[:, 0:n], ACT.Sqrt).then_inc(site[1], 1)

    def layer_norm(c, site, run, x, n, sq, gamma=None, beta=None, out=None):
        st_ = stat[:, 0:n]
        b3 = st_.unsqueeze(2).broadcast_to([P, n, H])
        c.link(nc.vector.tensor_reduce(st_, x, AX, ALU.add))
        c.link(nc.vector.tensor_single_scalar(st_, st_, -1.0 / H, ALU.mult))
        c.link(nc.vector.tensor_tensor(x, x, b3, ALU.add))
        c.link(nc.vector.tensor_tensor(sq, x, x, ALU.mult))
        c.link(nc.vector.tensor_reduce(st_, sq, AX, ALU.add))
        nc.vector.tensor_scalar(st_, st_, 1.0 / H, 1e-5, ALU.mult, ALU.add).then_inc(site[0], 1)
        c.eng.wait_ge(site[0], run + 1)
        c.eng.wait_ge(site[1], run + 1)
        c.link(nc.vector.reciprocal(st_, st_))
        out = x if out is None else out
        c.link(nc.vector.tensor_tensor(x if gamma is not None else out, x, b3, ALU.mult))
        if gamma is not None:
            c.link(nc.vector.tensor_tensor(x, x, gamma.unsqueeze(1).broadcast_to([P, n, H]), ALU.mult))
            c.end(nc.vector.tensor_tensor(out, x, beta.unsqueeze(1).broadcast_to([P, n, H]), ALU.add))

    def sq_view(n):
        return sq_all[:, 0:n * H].rearrange("p (n f) -> p n f", f=H)

    qn = xv48
    nrow = sq_all[:, 0:NB * 2 * H].rearrange("p (n f) -> p n f", f=2 * H)
    with ExitStack() as ctx:
        emb = sb("emb", [P, GF], F32, ctx)
        embT = sb("embT", [GF, P], F32, ctx)
        adapt = sb("adapt", [GF, GF], F32, ctx)
        ee = sb("ee", [P, 2 * GF], F32, ctx)
        typ = sb("typ", [P, NB], I32, ctx)
        mul = sb("mul", [P, NB], F32, ctx)
        eg = sb("eg", [P, NB, 2 * GF], F32, ctx)
        block = ctx.enter_context(nc.Block())

        @block.sync
        def _(sp):
            sp.dma_start(emb[0:NELEM, :], a["emb"]).then_inc(sem_rows, 16)
            sp.dma_start(adapt[:, :], a["adapt"]).then_inc(sem_rows, 16)
            sp.dma_start(typ[:, :], a["type_nodes"]).then_inc(sem_rows, 16)
            sp.dma_start(mul[:, :], a["mult_nodes"]).then_inc(sem_rows, 16)
            sp.dma_start(hc[:, :, 0:H], a["x_nodes"]).then_inc(sem_rows, 16)
            sp.dma_start(f1w[:, :], a["f1w"]).then_inc(sem_rows, 16)
            sp.dma_start(f1b[:, :], a["f1b"]).then_inc(sem_rows, 16)
            sp.dma_start(f2[:, :], a["f2"]).then_inc(sem_rows, 16)
            sp.dma_start(gn[:, :, :], a["gnbn"].rearrange("(o a) f -> o a f", o=1).broadcast_to([P, 2, H])
                         ).then_inc(sem_rows, 16)
            sp.dma_start(first_key[:, :], edges.rearrange("(p t) f -> p t f", p=P)[:, 0, C_SRC:C_SRC + 1].bitcast(I32),
                         allow_slow_non_contiguous=True).then_inc(sem_rows, 16)
            sp.wait_ge(emb_sb, 2)
            sp.dma_start(elems, ee[0:NELEM, :]).then_inc(ee_dma, 16)
            sp.wait_ge(ee_dma, 16)

        @block.tensor
        def _(pe):
            pe.wait_ge(sem_rows, 160)
            nc.tensor.transpose(bank[0][0:GF, 0:NELEM], emb[0:NELEM, :], ident[0:NELEM, 0:NELEM]).then_inc(emb_ps, 1)
            pe.wait_ge(emb_sb, 1)
            nc.tensor.matmul(bank[1][0:NELEM, 0:GF], embT[:, 0:NELEM], adapt[:, :], start=True, stop=True
                             ).then_inc(emb_ps, 1)

        @block.gpsimd
        def _(pool):
            pool.wait_ge(ee_dma, 16)
            for j in range(NB):
                nc.gpsimd.indirect_dma_start(out=eg[:, j, :], out_offset=None, in_=elems,
                                             in_offset=bass.IndirectOffsetOnAxis(ap=typ[:, j:j + 1], axis=0)
                                             ).then_inc(ee_rows, 16)

        @block.vector
        def _(dve):
            c = Chain(dve, setup_chain)
            for h in range(2):
                for name in ("rows_used", "g_used", "qi_ready", "prod_done", "so_ready"):
                    nc.vector.sem_inc(PS[name][h], 1)
            for h in range(2):
                c.link(nc.vector.memset(cf[h][:, :, 0], 0.0))
                c.link(nc.vector.memset(ce[h][:, :, 0], 0.0))
                c.link(nc.vector.memset(so[h][:, :, :], 0.0))
            c.link(nc.vector.memset(hid[:, :], 1.0))
            c.link(nc.vector.memset(wu[:, :], 0.0))
            c.link(nc.vector.memset(hc[:, :, H:HC], 0.0))
            c.link(nc.vector.memset(qn[:, :, :], 0.0))
            c.link(nc.vector.memset(nrow[:, :, :], 0.0))
            for tile, value in ((qc, 0.0), (vc, 0.0), (mc, 0.0), (kc, -1.0), (prevf, -1.0)):
                c.link(nc.vector.memset(tile[:, :], value))
            dve.wait_ge(sem_rows, 160)
            c.link(nc.vector.tensor_copy(ee[0:NELEM, 0:GF], emb[0:NELEM, :]))
            dve.wait_ge(emb_ps, 1)
            nc.vector.tensor_copy(embT[:, 0:NELEM], bank[0][0:GF, 0:NELEM]).then_inc(emb_sb, 1)
            dve.wait_ge(emb_ps, 2)
            nc.vector.tensor_copy(ee[0:NELEM, GF:2 * GF], bank[1][0:NELEM, 0:GF]).then_inc(emb_sb, 1)
            c.link(nc.vector.tensor_copy(nrow[:, :, GF], mul[:, :]))
            c.link(nc.vector.tensor_copy(nrow[:, :, H:2 * H], hc[:, :, 0:H]))
            dve.wait_ge(ee_rows, 16 * NB)
            c.link(nc.vector.tensor_copy(qn[:, :, 0:GF], eg[:, :, 0:GF]))
            c.link(nc.vector.tensor_copy(nrow[:, :, 0:GF], eg[:, :, GF:2 * GF]))

    def publish(tag, run, src_rows, parts, sems):
        table, scattered, began, begun = sems
        node_v = nodes.rearrange("(n p) f -> p n f", p=P)
        q_v = qnodes.rearrange("(n p) f -> p n f", p=P)
        n_dma = len(parts) + 1
        with ExitStack() as ctx:
            block = ctx.enter_context(nc.Block())

            @block.sync
            def _(sp):
                for cols, values in parts:
                    sp.dma_start(node_v[:, :, cols], values).then_inc(table, 16)
                sp.dma_start(q_v, src_rows).then_inc(table, 16)
                sp.wait_ge(began, 16 * run + 16)
                sp.wait_ge(scattered, 16 * NB * run + 16 * NB)
                sp.dma_start(fill[0:S, :].rearrange("(p t) f -> p t f", p=P)[:, 0, :], q0[:, :]).then_inc(begun, 16)
                sp.wait_ge(begun, 16 * run + 16)
                nc.sync.sem_inc(go, 1)

            @block.gpsimd
            def _(pool):
                for j in range(NB):
                    nc.gpsimd.indirect_dma_start(
                        out=fill, out_offset=bass.IndirectOffsetOnAxis(ap=first_i[:, j:j + 1], axis=0),
                        in_=src_rows[:, j, :], in_offset=None).then_inc(scattered, 16)
                pool.wait_ge(table, 16 * n_dma * run + 16 * n_dma)
                nc.gpsimd.sem_inc(go, 1)
                nc.gpsimd.indirect_dma_start(
                    out=q0[:, :], out_offset=None, in_=qnodes,
                    in_offset=bass.IndirectOffsetOnAxis(ap=first_key[:, 0:1], axis=0)).then_inc(began, 16)

    def publish_sems(kind):
        return [sem(f"{n}_{kind}") for n in ("table", "scattered", "began", "begun")]

    publish("init", 0, qn, ((slice(0, 2 * H), nrow),), publish_sems("init"))

    def edge_pass(kind, run):
        m = PS
        done = {"init": 0, "layer": run + 1, "nbr": L + 1}[kind]
        keyed_done = {"init": 0, "layer": 0, "nbr": 1}[kind]
        rows_v = (bydst if kind == "nbr" else edges).rearrange("(p t) f -> p t f", p=P)
        fill_v = fill[0:S, :].rearrange("(p t) f -> p (t f)", p=P)
        state_v = state[0:S, :].rearrange("(p t) f -> p t f", p=P)
        keyed = kind in ("init", "nbr")
        rbuf = pair_i if kind == "nbr" else ea
        with ExitStack() as ctx:
            block = ctx.enter_context(nc.Block())

            @block.sync
            def _(sp):
                with sp.Fori(0, PAIRS) as i:
                    for h in range(2):
                        n = done * PAIRS + i + 1
                        k = 2 * i + h
                        sp.wait_ge(m["rows_used"][h], n)
                        sp.dma_start(rbuf[h][:, :, :], rows_v[:, bass.ds(k * TC, TC), :]
                                     ).then_inc(m["row_landed"][h], 16)
                        if kind != "nbr":
                            sp.wait_ge(m["qi_ready"][h], n)
                            sp.dma_start(pf_all[:, 2 + h, :], fill_v[:, bass.ds(k * (TC * H), TC * H)]
                                         ).then_inc(m["fill_landed"][h], 16)

            @block.gpsimd
            def _(pool):
                with pool.Fori(0, PAIRS) as i:
                    for h in range(2):
                        n = done * PAIRS + i + 1
                        pool.wait_ge(m["row_landed"][h], 16 * n)
                        pool.wait_ge(m["g_used"][h], n)
                        nc.gpsimd.sem_inc(go, 1)
                        for t in range(TC):
                            if kind == "nbr":
                                idx, src, out = pair_i[h][:, t, 0:1], qnodes, g_all[:, h, t, 0:H]
                            else:
                                idx = ea[h][:, t, C_DST:C_DST + 1].bitcast(I32)
                                src, out = nodes, g_all[:, h, t, :]
                            nc.gpsimd.indirect_dma_start(
                                out=out, out_offset=None, in_=src,
                                in_offset=bass.IndirectOffsetOnAxis(ap=idx, axis=0)
                            ).then_inc(m["g_landed", kind][h], 16)

            @block.scalar
            def _(act):
                with act.Fori(0, PAIRS) as i:
                    for h in range(2):
                        n = done * PAIRS + i + 1
                        k = 2 * i + h
                        act.wait_ge(m["prod_done"][h], n)
                        if keyed:
                            act.wait_ge(m["flags_ready"][h], keyed_done * PAIRS + i + 1)
                        nc.scalar.copy(cf[h][:, :, 1:TC + 1],
                                       same[:, bass.ds(k * TC, TC)].unsqueeze(1).broadcast_to([P, H + 1, TC])
                                       ).then_inc(m["cf_ready"][h], 1)
                        if kind != "nbr":
                            act.wait_ge(m["fill_landed"][h], 16 * n)
                            nc.scalar.copy(qi[h][:, :, 1:TC + 1],
                                           pf_all[:, 2 + h, :].rearrange("p (t f) -> p f t", f=H)
                                           ).then_inc(m["qi_ready"][h], 1)
                        if kind == "init":
                            for q in range(GQ):
                                gg = (2 * GQ) * i + GQ * h + q + 1
                                act.wait_ge(et_ready, gg)
                                nc.scalar.copy(eaT[q % 2][:, :], bank[q % 2][0:RBF, :]).then_inc(eat_ready, 1)
                                act.wait_ge(hp_ready, gg)
                                nc.scalar.activation(hid[0:H, :], bank[2][0:H, :], ACT.Silu, bias=f1b[:, 0:1]
                                                     ).then_inc(hid_ready, 1)
                        if kind == "layer":
                            act.wait_ge(m["s_ready"][h], run * PAIRS + i + 1)
                            nc.scalar.activation(es[h][:, :], d2[h][:, :], ACT.Exp)
                            nc.scalar.activation(ce[h][:, :, 1:TC + 1],
                                                 d1[h][:, :].unsqueeze(1).broadcast_to([P, H + 1, TC]), ACT.Exp
                                                 ).then_inc(m["coef_ready"][h], 1)
                        act.wait_ge(m["v_done"][h], n)
                        w = H if kind == "nbr" else H + 1
                        if kind == "layer":
                            nc.scalar.copy(so[h][:, :, H + 1], mx[h][:, 1:TC + 1])
                        nc.scalar.copy(so[h][:, :, 0:w].rearrange("p t f -> p f t"), v[h][:, 0:w, 1:TC + 1]
                                       ).then_inc(m["so_ready"][h], 1)
                        act.wait_ge(m["so_ready"][h], n + 1)
                        act.dma_start(state_v[:, bass.ds(k * TC, TC), :], so[h][:, :, :]
                                      ).then_inc(m["so_stored"][h], 16)
                    for h in range(2):
                        act.wait_ge(m["so_stored"][h], 16 * (done * PAIRS + i + 1))

            if kind == "init":
                @block.tensor
                def _(pe):
                    with pe.Fori(0, PAIRS) as i:
                        for h in range(2):
                            pe.wait_ge(m["row_landed"][h], 16 * i + 16)
                            nc.tensor.sem_inc(pe_go, 1)
                            for q in range(GQ):
                                gg = (2 * GQ) * i + GQ * h + q + 1
                                for j in range(4):
                                    ins = nc.tensor.transpose(bank[q % 2][0:RBF, j * P:(j + 1) * P],
                                                              ea[h][:, 4 * q + j, 0:RBF], ident[:, :])
                                ins.then_inc(et_ready, 1)
                                pe.wait_ge(eat_ready, gg)
                                nc.tensor.sem_inc(pe_go, 1)
                                nc.tensor.matmul(bank[2][0:H, :], f1w[:, :], eaT[q % 2][:, :], start=True,
                                                 stop=True).then_inc(hp_ready, 1)
                                pe.wait_ge(hid_ready, gg)
                                nc.tensor.sem_inc(pe_go, 1)
                                if q == 0:
                                    pe.wait_ge(gate_read, 2 * i + h + 1)
                                    nc.tensor.sem_inc(pe_go, 1)
                                for j in range(4):
                                    t = 4 * q + j
                                    o = (t % GATE_BANK) * H
                                    ins = nc.tensor.matmul(bank[3 + t // GATE_BANK][:, o:o + H],
                                                           hid[0:H + 1, j * P:(j + 1) * P], f2[:, :],
                                                           start=True, stop=True)
                                if q == GQ - 1:
                                    ins.then_inc(gate_ready, 1)

            @block.vector
            def _(dve):
                if kind == "init":
                    nc.vector.sem_inc(gate_read, 1)
                per = {"init": 20, "layer": 30, "nbr": 4}[kind]
                with dve.Fori(0, PAIRS) as i:
                    c = Chain(dve, m["chain", kind], (run * PAIRS + i) * per)
                    for h in range(2):
                        n = done * PAIRS + i + 1
                        k = 2 * i + h
                        gh = g_all[:, h, :, :]
                        prod = pf_all[:, h, :].rearrange("p (t f) -> p t f", f=H)
                        dve.wait_ge(m["row_landed"][h], 16 * n)
                        if keyed:
                            keys = pair_i[h][:, :, 1] if kind == "nbr" else ea[h][:, :, C_SRC + 1]
                            nc.vector.tensor_copy(srcf[:, bass.ds(k * TC, TC)], keys)
                            nc.vector.tensor_copy(k1[h][:, 0:1], kc[:, :])
                            c.link(nc.vector.tensor_copy(k1[h][:, 1:TC + 1], keys))
                            nc.vector.tensor_copy(kc[:, :], k1[h][:, TC:TC + 1])
                            nc.vector.tensor_tensor(same[:, bass.ds(k * TC, TC)], k1[h][:, 1:TC + 1],
                                                    k1[h][:, 0:TC], ALU.is_equal).then_inc(m["flags_ready"][h], 1)
                        if kind == "layer":
                            dve.wait_ge(m["g_landed", kind][h], 16 * TC * (run * PAIRS + i + 1))
                            nc.vector.scalar_tensor_tensor(gh[:, :, 0:RBF], ea[h][:, :, 0:RBF], 0.1,
                                                           gh[:, :, 0:RBF], ALU.mult, ALU.add
                                                           ).then_inc(m["rows_used"][h], 1)
                        if kind != "nbr":
                            dve.wait_ge(m["qi_ready"][h], n + 1)
                            dve.wait_ge(m["cf_ready"][h], n)
                            c.link(nc.vector.tensor_copy(qi[h][:, :, 0], qc[:, :]))
                            c.link(nc.vector.tensor_tensor_scan(flat(qi[h][:, :, :]), flat(cf[h][:, 0:H, :]),
                                                                flat(qi[h][:, :, :]), 0.0, ALU.mult, ALU.add))
                            c.link(nc.vector.tensor_copy(qc[:, :], qi[h][:, :, TC]))
                        if kind == "layer":
                            dve.wait_ge(m["rows_used"][h], n + 1)
                            c.link(nc.vector.tensor_tensor(
                                prod, qi[h][:, :, 1:TC + 1].rearrange("p f t -> p t f"), gh[:, :, 0:H], ALU.mult))
                            nc.vector.tensor_reduce(sc[h][:, :], prod, AX, ALU.add).then_inc(m["prod_done"][h], 1)
                            dve.wait_ge(m["prod_done"][h], n + 1)
                            c.link(nc.vector.tensor_tensor(sc[h][:, :], sc[h][:, :],
                                                           logm[:, bass.ds(k * TC, TC)], ALU.add))
                            c.link(nc.vector.tensor_scalar(pen[:, :], same[:, bass.ds(k * TC, TC)], BIG, -BIG,
                                                           ALU.mult, ALU.add))
                            dve.wait_ge(m["so_ready"][h], n)
                            c.link(nc.vector.tensor_copy(mx[h][:, 0:1], mc[:, :]))
                            c.link(nc.vector.tensor_tensor_scan(mx[h][:, 1:TC + 1], pen[:, :], sc[h][:, :],
                                                                mx[h][:, 0:1], ALU.add, ALU.max))
                            c.link(nc.vector.tensor_copy(mc[:, :], mx[h][:, TC:TC + 1]))
                            c.link(nc.vector.tensor_tensor(d1[h][:, :], mx[h][:, 0:TC], mx[h][:, 1:TC + 1],
                                                           ALU.subtract))
                            c.link(nc.vector.scalar_tensor_tensor(d1[h][:, :], d1[h][:, :], 0.0, pen[:, :],
                                                                  ALU.min, ALU.add))
                            c.link(nc.vector.tensor_tensor(d2[h][:, :], sc[h][:, :], mx[h][:, 1:TC + 1],
                                                           ALU.subtract))
                            nc.vector.tensor_single_scalar(d2[h][:, :], d2[h][:, :], 20.0, ALU.min
                                                           ).then_inc(m["s_ready"][h], 1)
                            dve.wait_ge(m["coef_ready"][h], run * PAIRS + i + 1)
                            c.link(nc.vector.tensor_copy(v[h][:, H, 1:TC + 1], es[h][:, :]))
                            nc.vector.tensor_tensor(
                                v[h][:, 0:H, 1:TC + 1], gh[:, :, H:2 * H].rearrange("p t f -> p f t"),
                                es[h][:, :].unsqueeze(1).broadcast_to([P, H, TC]), ALU.mult
                            ).then_inc(m["g_used"][h], 1)
                            coef = ce
                        elif kind == "init":
                            dve.wait_ge(m["g_landed", kind][h], 16 * TC * (run * PAIRS + i + 1))
                            c.link(nc.vector.tensor_tensor(
                                prod[:, :, 0:GF], qi[h][:, 0:GF, 1:TC + 1].rearrange("p f t -> p t f"),
                                gh[:, :, 0:GF], ALU.mult))
                            c.link(nc.vector.tensor_reduce(sc[h][:, :], prod[:, :, 0:GF], AX, ALU.add))
                            c.link(nc.vector.tensor_copy(logm[:, bass.ds(k * TC, TC)], gh[:, :, GF]))
                            dve.wait_ge(gate_ready, 2 * i + h + 1)
                            nc.vector.tensor_tensor(es[h][:, :], ea[h][:, :, C_CW], gh[:, :, GF], ALU.mult
                                                    ).then_inc(m["rows_used"][h], 1)
                            for b in range(-(-TC // GATE_BANK)):
                                t0, t1 = b * GATE_BANK, min(TC, (b + 1) * GATE_BANK)
                                ins = nc.vector.tensor_tensor(
                                    prod[:, t0:t1, :],
                                    bank[3 + b][:, 0:(t1 - t0) * H].rearrange("p (t f) -> p t f", f=H),
                                    sc[h][:, t0:t1].unsqueeze(2).broadcast_to([P, t1 - t0, H]), ALU.add)
                            ins.then_inc(gate_read, 1)
                            dve.wait_ge(gate_read, 2 * i + h + 2)
                            c.link(nc.vector.tensor_tensor(prod, prod, gh[:, :, H:2 * H], ALU.mult))
                            dve.wait_ge(m["so_ready"][h], n)
                            c.link(nc.vector.tensor_copy(v[h][:, H, 1:TC + 1], gh[:, :, GF]))
                            nc.vector.tensor_tensor(
                                v[h][:, 0:H, 1:TC + 1], prod.rearrange("p t f -> p f t"),
                                es[h][:, :].unsqueeze(1).broadcast_to([P, H, TC]), ALU.mult
                            ).then_inc(m["g_used"][h], 1)
                            coef = cf
                        else:
                            dve.wait_ge(m["g_landed", kind][h], 16 * TC * (run * PAIRS + i + 1))
                            dve.wait_ge(m["so_ready"][h], n)
                            dve.wait_ge(m["flags_ready"][h], keyed_done * PAIRS + i + 1)
                            nc.vector.tensor_copy(v[h][:, 0:H, 1:TC + 1],
                                                  gh[:, :, 0:H].rearrange("p t f -> p f t")
                                                  ).then_inc(m["g_used"][h], 1)
                            dve.wait_ge(m["cf_ready"][h], n)
                            nc.vector.sem_inc(m["rows_used"][h], 1)
                            coef = cf
                        w = H if kind == "nbr" else H + 1
                        c.link(nc.vector.tensor_copy(v[h][:, 0:w, 0], vc[:, 0:w]))
                        dve.wait_ge(m["g_used"][h], n + 1)
                        nc.vector.tensor_tensor_scan(flat(v[h][:, 0:w, :]), flat(coef[h][:, 0:w, :]),
                                                     flat(v[h][:, 0:w, :]), 0.0, ALU.mult, ALU.add
                                                     ).then_inc(m["v_done"][h], 1)
                        dve.wait_ge(m["v_done"][h], n)
                        if keyed:
                            nc.vector.tensor_copy(vc[:, 0:w], v[h][:, 0:w, TC]).then_inc(m["prod_done"][h], 1)
                            dve.wait_ge(m["prod_done"][h], n + 1)
                        else:
                            c.link(nc.vector.tensor_copy(vc[:, 0:w], v[h][:, 0:w, TC]))
                    c.last(per)

    GQ = TC // 4
    et_ready, eat_ready, hp_ready = sem("et_ready"), sem("eat_ready"), sem("hp_ready")
    hid_ready, gate_ready, gate_read = sem("hid_ready"), sem("gate_ready"), sem("gate_read")

    def crossings(tag):
        with ExitStack() as ctx:
            chain, shifted, wanted, turned = (sem(f"{n}_{tag}") for n in
                                              ("cross_chain", "shifted", "last_ready", "cross_ps"))
            block = ctx.enter_context(nc.Block())

            @block.sync
            def _(sp):
                sp.wait_ge(wanted, 1)
                sp.dma_start(prevf[1:P, :], lastf[0:P - 1, :]).then_inc(shifted, 16)
                sp.wait_ge(shifted, 16)

            @block.tensor
            def _(pe):
                pe.wait_ge(wanted, 2)
                nc.tensor.matmul(bank[0][0:H + 1, 0:P], ones[:, 0:H + 1], diag[:, :], start=True, stop=True
                                 ).then_inc(turned, 1)

            @block.vector
            def _(dve):
                c = Chain(dve, chain)
                c.link(nc.vector.memset(mc[:, :], 0.0))
                nc.vector.tensor_copy(lastf[:, :], srcf[:, T - 1:T]).then_inc(wanted, 1)
                if tag == "init":
                    c.link(nc.vector.tensor_single_scalar(logm[:, :], logm[:, :], 1.0, ALU.max))
                dve.wait_ge(shifted, 16)
                dve.wait_ge(wanted, 1)
                c.link(nc.vector.tensor_tensor(cont[:, :], srcf[:, 0:1], prevf[:, :], ALU.is_equal))
                c.link(nc.vector.tensor_tensor(fix_f[:, :], lastf[:, :], prevf[:, :], ALU.is_equal))
                nc.vector.tensor_scalar(diag[:, :], ident[:, :], fix_f[:, 0:1], None, ALU.mult).then_inc(wanted, 1)
                dve.wait_ge(wanted, 2)
                junk = sq_all[:, 0:T]
                c.link(nc.vector.tensor_scalar(junk, srcf[:, :], srcf[:, 0:1], None, ALU.is_equal))
                c.link(nc.vector.tensor_reduce(nrun[:, :], junk, AX, ALU.add))
                c.link(nc.vector.tensor_scalar(fix_f[:, :], pidx[:, :], float(T - 1), -1.0 - S, ALU.mult, ALU.add))
                c.link(nc.vector.tensor_tensor(fix_f[:, :], fix_f[:, :], nrun[:, :], ALU.add))
                c.link(nc.vector.tensor_tensor(fix_f[:, :], fix_f[:, :], cont[:, :], ALU.mult))
                c.link(nc.vector.tensor_tensor(fix_f[:, :], fix_f[:, :], pidx[:, :], ALU.add))
                c.link(nc.vector.tensor_single_scalar(fix_f[:, :], fix_f[:, :], float(S), ALU.add))
                c.link(nc.vector.tensor_copy(fix_i[:, :], fix_f[:, :]))
                dve.wait_ge(turned, 1)
                c.link(nc.vector.tensor_copy(chb[:, :], bank[0][0:H + 1, 0:P]))
                c.link(nc.vector.tensor_scalar(penc[:, :], chb[:, :], BIG, -BIG, ALU.mult, ALU.add))

            if tag == "init":
                @block.scalar
                def _(act):
                    act.wait_ge(chain, 2)
                    nc.scalar.activation(logm[:, :], logm[:, :], ACT.Ln)

    def finish(tag, run, key, sems):
        chain, parts, ps_ok, ex, fixed, sent, got = sems
        per = 12
        with ExitStack() as ctx:
            block = ctx.enter_context(nc.Block())

            @block.gpsimd
            def _(pool):
                nc.gpsimd.indirect_dma_start(
                    out=fx[:, :], out_offset=None, in_=state,
                    in_offset=bass.IndirectOffsetOnAxis(ap=fix_i[:, 0:1], axis=0)).then_inc(fixed, 16)
                pool.wait_ge(parts, 4 * run + 4)
                nc.gpsimd.sem_inc(go, 1)
                nc.gpsimd.indirect_dma_start(
                    out=state, out_offset=bass.IndirectOffsetOnAxis(ap=fix_i[:, 0:1], axis=0),
                    in_=fx[:, :], in_offset=None).then_inc(sent, 16)
                pool.wait_ge(sent, 16 * run + 16)
                nc.gpsimd.sem_inc(go, 1)
                for j in range(NB):
                    nc.gpsimd.indirect_dma_start(
                        out=ns[:, j, :], out_offset=None, in_=state,
                        in_offset=bass.IndirectOffsetOnAxis(ap=last_i[key][:, j:j + 1], axis=0)).then_inc(got, 16)

            @block.sync
            def _(sp):
                sp.wait_ge(got, 16 * NB * run + 16 * NB)
                nc.sync.sem_inc(go, 1)

            @block.tensor
            def _(pe):
                pe.wait_ge(parts, 4 * run + 1)
                nc.tensor.sem_inc(pe_go, 1)
                nc.tensor.transpose(bank[0][0:H + 1, 0:P], vc[:, :], ident[:, :])
                nc.tensor.matmul(bank[1][0:H + 1, 0:P], ones[:, 0:H + 1], diag[:, :], start=True, stop=True
                                 ).then_inc(ps_ok, 1)
                pe.wait_ge(parts, 4 * run + 3)
                nc.tensor.sem_inc(pe_go, 1)
                nc.tensor.transpose(bank[2][:, 0:H + 1], vcar[:, 0:P], ident[0:H + 1, 0:H + 1])
                nc.tensor.transpose(bank[3][:, 0:H + 1], mcar[:, 0:P], ident[0:H + 1, 0:H + 1]).then_inc(ps_ok, 1)

            @block.scalar
            def _(act):
                act.wait_ge(parts, 4 * run + 2)
                nc.scalar.activation(arg[:, :], arg[:, :], ACT.Exp).then_inc(ex, 1)
                act.wait_ge(chain, per * run + 9)
                nc.scalar.activation(fa[:, :], fa[:, :], ACT.Exp).then_inc(ex, 1)

            @block.vector
            def _(dve):
                c = Chain(dve, chain, per * run)
                nc.vector.tensor_scalar(diag[:, :], ident[:, :], mc[:, 0:1], None, ALU.mult).then_inc(parts, 1)
                c.link(nc.vector.memset(mcar[:, 0:1], -BIG))
                c.link(nc.vector.memset(vcar[:, 0:1], 0.0))
                dve.wait_ge(ps_ok, 2 * run + 1)
                c.link(nc.vector.tensor_copy(mr[:, :], bank[1][0:H + 1, 0:P]))
                c.link(nc.vector.tensor_tensor_scan(mcar[:, 1:P + 1], penc[:, :], mr[:, :], -BIG, ALU.add, ALU.max))
                c.link(nc.vector.tensor_tensor(arg[:, 0:P], mr[:, :], mcar[:, 1:P + 1], ALU.subtract))
                c.link(nc.vector.tensor_tensor(arg[:, P:2 * P], mcar[:, 0:P], mcar[:, 1:P + 1], ALU.subtract))
                nc.vector.scalar_tensor_tensor(arg[:, P:2 * P], arg[:, P:2 * P], 0.0, penc[:, :], ALU.min, ALU.add
                                               ).then_inc(parts, 1)
                dve.wait_ge(ex, 2 * run + 1)
                c.link(nc.vector.tensor_tensor(mr[:, :], arg[:, 0:P], bank[0][0:H + 1, 0:P], ALU.mult))
                nc.vector.tensor_tensor_scan(vcar[:, 1:P + 1], arg[:, P:2 * P], mr[:, :], 0.0, ALU.mult, ALU.add
                                             ).then_inc(parts, 1)
                dve.wait_ge(ps_ok, 2 * run + 2)
                dve.wait_ge(fixed, 16 * run + 16)
                c.link(nc.vector.tensor_tensor(fm[:, :], fx[:, H + 1:ST], bank[3][:, 0:1], ALU.max))
                nc.vector.tensor_tensor(fa[:, 0:1], fx[:, H + 1:ST], fm[:, :], ALU.subtract)
                c.link(nc.vector.tensor_tensor(fa[:, 1:2], bank[3][:, 0:1], fm[:, :], ALU.subtract))
                dve.wait_ge(ex, 2 * run + 2)
                c.link(nc.vector.tensor_tensor(fa[:, 1:2], fa[:, 1:2], cont[:, :], ALU.mult))
                c.link(nc.vector.tensor_scalar(fx[:, 0:H + 1], fx[:, 0:H + 1], fa[:, 0:1], None, ALU.mult))
                c.link(nc.vector.scalar_tensor_tensor(fx[:, 0:H + 1], bank[2][:, 0:H + 1], fa[:, 1:2],
                                                      fx[:, 0:H + 1], ALU.mult, ALU.add))
                nc.vector.tensor_copy(fx[:, H + 1:ST], fm[:, :]).then_inc(parts, 1)
                c.last(per)

    def finish_sems(kind):
        return [sem(f"{n}_{kind}") for n in ("fin_chain", "parts", "fin_ps", "fin_exp", "fix_got", "fix_sent", "ns_got")]

    edge_pass("init", 0)
    crossings("init")
    finish("init", 0, 0, finish_sems("init"))

    upd_chain = sem("upd_chain")
    upd_root = root_site("upd")
    with ExitStack() as ctx:
        block = ctx.enter_context(nc.Block())

        @block.scalar
        def _(act):
            take_root(act, upd_root, 0, NB)

        @block.vector
        def _(dve):
            c = Chain(dve, upd_chain)
            inv = stat[:, NB:2 * NB]
            c.link(nc.vector.tensor_single_scalar(inv, ns[:, :, H], 1e-8, ALU.max))
            c.link(nc.vector.reciprocal(inv, inv))
            c.link(nc.vector.tensor_tensor(xv48, ns[:, :, 0:H], inv.unsqueeze(2).broadcast_to([P, NB, H]), ALU.mult))
            c.link(nc.vector.tensor_tensor(xv48, xv48, hc[:, :, 0:H], ALU.add))
            layer_norm(c, upd_root, 0, xv48, NB, sq_view(NB), gn[:, 0, :], gn[:, 1, :], hc[:, :, 0:H])

    def node_product(pe, act, dve, run, rows, rhs, width, out, sems):
        tp_ready, ht_ready, op_ready, op_read = sems
        groups = [(q, min(4, NB - 4 * q)) for q in range(NGRP)]
        r = run * NGRP
        if pe is not None:
            def turn(q, k):
                for j in range(k):
                    ins = nc.tensor.transpose(bank[q % 2][0:rows, j * P:(j + 1) * P], hc[:, 4 * q + j, 0:rows],
                                              ident[:, :])
                ins.then_inc(tp_ready, 1)

            turn(*groups[0])
            for q, k in groups:
                if q + 1 < NGRP:
                    turn(*groups[q + 1])
                pe.wait_ge(ht_ready, r + q + 1)
                nc.tensor.sem_inc(pe_go, 1)
                if q >= 2:
                    pe.wait_ge(op_read, r + q - 1)
                    nc.tensor.sem_inc(pe_go, 1)
                for j in range(k):
                    ins = nc.tensor.matmul(bank[2 + q % 2][:, j * width:(j + 1) * width],
                                           htg[q % 2][0:rows, j * P:(j + 1) * P], rhs, start=True, stop=True)
                ins.then_inc(op_ready, 1)
        if act is not None:
            for q, k in groups:
                act.wait_ge(tp_ready, r + q + 1)
                if q >= 2:
                    act.wait_ge(op_ready, r + q - 1)
                nc.scalar.copy(htg[q % 2][0:rows, 0:k * P], bank[q % 2][0:rows, 0:k * P]).then_inc(ht_ready, 1)
        if dve is not None:
            for q, k in groups:
                dve.wait_ge(op_ready, r + q + 1)
                nc.vector.tensor_copy(out[:, 4 * q:4 * q + k, :],
                                      bank[2 + q % 2][:, 0:k * width].rearrange("p (n f) -> p n f", f=width)
                                      ).then_inc(op_read, 1)
            dve.wait_ge(op_read, r + NGRP)

    w_dma, w_ok, w_sb = sem("w_dma"), sem("w_ok"), sem("w_sb")
    qk_sems = [sem(n) for n in ("q_tp", "q_ht", "q_op", "q_read")]
    up_sems = [sem(n) for n in ("u_tp", "u_ht", "u_op", "u_read")]
    qk_chain, lay_chain = sem("qk_chain"), sem("lay_chain")
    qk_root, lay_root = root_site("qk"), root_site("lay")
    pub = publish_sems("layer")
    fin = finish_sems("layer")
    with nc.Fori(0, L) as l:
        with ExitStack() as ctx:
            block = ctx.enter_context(nc.Block())

            @block.sync
            def _(sp):
                for out, src in ((wqk, a["wqk"]), (wmT, a["wmT"])):
                    sp.dma_start(out[:, :], src[bass.ds(l, 1), :, :].rearrange("o k f -> (o k) f")).then_inc(w_dma, 16)
                wu_l = a["wu"][bass.ds(l, 1), :, :].rearrange("o k f -> (o k) f")
                sp.dma_start(wu[0:H, :], wu_l[0:H, :]).then_inc(w_dma, 16)
                sp.dma_start(wub[:, :], wu_l[H:2 * H, :]).then_inc(w_dma, 16)
                sp.dma_start(gb[:, :, :], a["scales"][bass.ds(l, 1), :, :].broadcast_to([P, 6, H])).then_inc(w_dma, 16)

            @block.tensor
            def _(pe):
                pe.wait_ge(w_dma, 80 * l + 80)
                nc.tensor.sem_inc(pe_go, 1)
                nc.tensor.matmul(bank[4][OFF:OFF + H, 0:H], wmT[:, :], wub[:, :], start=True, stop=True
                                 ).then_inc(w_ok, 1)
                node_product(pe, None, None, l, H, wqk[:, :], 2 * H, xv96, qk_sems)

            @block.scalar
            def _(act):
                act.wait_ge(w_ok, l + 1)
                nc.scalar.copy(wu[OFF:OFF + H, :], bank[4][OFF:OFF + H, 0:H]).then_inc(w_sb, 1)
                node_product(None, act, None, l, H, None, 2 * H, xv96, qk_sems)
                take_root(act, qk_root, l, 2 * NB)

            @block.vector
            def _(dve):
                c = Chain(dve, qk_chain, 14 * l)
                c.link(nc.vector.memset(mc[:, :], -BIG))
                c.link(nc.vector.memset(vc[:, :], 0.0))
                c.link(nc.vector.memset(qc[:, :], 0.0))
                node_product(None, None, dve, l, H, None, 2 * H, xv96, qk_sems)
                dve.wait_ge(w_dma, 80 * l + 80)
                both = x2[:, 0:NB * 2 * H].rearrange("p (n f) -> p n f", f=H)
                layer_norm(c, qk_root, l, both, 2 * NB, sq_all[:, 0:2 * NB * H].rearrange("p (n f) -> p n f", f=H))
                x4 = x2[:, 0:NB * 2 * H].rearrange("p (n o f) -> p n o f", o=2, f=H)
                for o in range(2):
                    c.link(nc.vector.tensor_tensor(x4[:, :, o, :], x4[:, :, o, :],
                                                   gb[:, o, :].unsqueeze(1).broadcast_to([P, NB, H]), ALU.mult))
                    c.end(nc.vector.tensor_tensor(x4[:, :, o, :], x4[:, :, o, :],
                                                  gb[:, 2 + o, :].unsqueeze(1).broadcast_to([P, NB, H]), ALU.add))
                c.last(14)

        publish("layer", l, xv96[:, :, 0:H],
                ((slice(0, H), xv96[:, :, H:2 * H]), (slice(H, 2 * H), hc[:, :, 0:H])), pub)
        edge_pass("layer", l)
        finish("layer", l, 0, fin)
        with ExitStack() as ctx:
            block = ctx.enter_context(nc.Block())

            @block.tensor
            def _(pe):
                pe.wait_ge(lay_chain, 14 * l + 3)
                nc.tensor.sem_inc(pe_go, 1)
                node_product(pe, None, None, l, HC, wu[:, :], H, xv48, up_sems)

            @block.scalar
            def _(act):
                node_product(None, act, None, l, HC, None, H, xv48, up_sems)
                take_root(act, lay_root, l, NB)

            @block.vector
            def _(dve):
                c = Chain(dve, lay_chain, 14 * l)
                inv = stat[:, NB:2 * NB]
                c.link(nc.vector.tensor_single_scalar(inv, ns[:, :, H], 1e-10, ALU.add))
                c.link(nc.vector.reciprocal(inv, inv))
                c.link(nc.vector.tensor_tensor(hc[:, :, OFF:OFF + H], ns[:, :, 0:H],
                                               inv.unsqueeze(2).broadcast_to([P, NB, H]), ALU.mult))
                node_product(None, None, dve, l, HC, None, H, xv48, up_sems)
                c.link(nc.vector.scalar_tensor_tensor(flat(xv48), flat(xv48), 0.01, flat(xv48), ALU.mult, ALU.max))
                c.link(nc.vector.tensor_tensor(xv48, xv48, hc[:, :, 0:H], ALU.add))
                layer_norm(c, lay_root, l, xv48, NB, sq_view(NB), gb[:, 4, :], gb[:, 5, :], hc[:, :, 0:H])
                c.last(14)

    mid_chain, x_dma, r_dma = sem("mid_chain"), sem("x_dma"), sem("r_dma")
    mid_root, deg_root, end_root = root_site("mid"), root_site("deg"), root_site("end")
    x1 = hc[:, :, 0:H]
    xd = hc[:, :, OFF:OFF + H]
    with ExitStack() as ctx:
        block = ctx.enter_context(nc.Block())

        @block.sync
        def _(sp):
            sp.dma_start(xv48, a["x_nodes"]).then_inc(x_dma, 16)
            sp.wait_ge(mid_chain, 10)
            sp.dma_start(qnodes.rearrange("(n p) f -> p n f", p=P), xd).then_inc(r_dma, 16)
            sp.wait_ge(r_dma, 16)

        @block.scalar
        def _(act):
            take_root(act, mid_root, 0, NB)
            take_root(act, deg_root, 0, NB)

        @block.vector
        def _(dve):
            c = Chain(dve, mid_chain)
            dve.wait_ge(x_dma, 16)
            c.link(nc.vector.tensor_tensor(xv48, xv48, hc[:, :, 0:H], ALU.add))
            layer_norm(c, mid_root, 0, xv48, NB, sq_view(NB), out=x1)
            nc.vector.tensor_single_scalar(stat[:, 0:NB], count[0][:, :], 1.0, ALU.add).then_inc(deg_root[0], 1)
            dve.wait_ge(deg_root[1], 1)
            c.link(nc.vector.reciprocal(dis[:, :], stat[:, 0:NB]))
            c.link(nc.vector.tensor_tensor(xd, x1, dis[:, :].unsqueeze(2).broadcast_to([P, NB, H]), ALU.mult))
            c.link(nc.vector.memset(vc[:, :], 0.0))
            c.link(nc.vector.memset(kc[:, :], -1.0))
            for h in range(2):
                nc.vector.memset(so[h][:, :, H:ST], 0.0)

    edge_pass("nbr", 0)
    crossings("nbr")
    finish("nbr", 0, 1, finish_sems("nbr"))
    end_chain, out_dma = sem("end_chain"), sem("out_dma")
    with ExitStack() as ctx:
        block = ctx.enter_context(nc.Block())

        @block.scalar
        def _(act):
            take_root(act, end_root, 0, NB)

        @block.vector
        def _(dve):
            c = Chain(dve, end_chain)
            c.link(nc.vector.tensor_tensor(xv48, ns[:, :, 0:H], xd, ALU.add))
            c.link(nc.vector.tensor_tensor(xv48, xv48, dis[:, :].unsqueeze(2).broadcast_to([P, NB, H]), ALU.mult))
            c.link(nc.vector.tensor_tensor(xv48, xv48, x1, ALU.add))
            layer_norm(c, end_root, 0, xv48, NB, sq_view(NB))

        @block.sync
        def _(sp):
            sp.wait_ge(end_chain, 10)
            full = N // P
            sp.dma_start(a["out"][0:full * P, :].rearrange("(n p) f -> p n f", p=P), xv48[:, 0:full, :]
                         ).then_inc(out_dma, 16)
            sp.dma_start(a["out"][full * P:N, :], xv48[0:N - full * P, full, :]).then_inc(out_dma, 16)
            sp.wait_ge(out_dma, 32)


def kernel(**inputs):
    import numpy as np
    import concourse.bacc as bacc
    from concourse.bass_utils import run_bass_kernel_spmd as run

    def pad(x, n, value):
        x = np.asarray(x)
        return np.concatenate([x, np.full((n - x.shape[0],) + x.shape[1:], value, x.dtype)], axis=0)

    def node_cols(x, value):
        x = pad(x, NN, value).reshape((NB, P) + np.asarray(x).shape[1:])
        return np.ascontiguousarray(np.moveaxis(x, 0, 1))

    w = {k[7:]: np.ascontiguousarray(v) for k, v in inputs.items() if k.startswith("L0_gnn_")}
    arrays = {
        "edge_attr": pad(inputs["edge_attr_40"], S, 0),
        "edge_weight": pad(inputs["edge_weight"], S, 0).reshape(P, T),
        "x_nodes": node_cols(inputs["x"], 0),
        "mult_nodes": node_cols(inputs["node_vec"], 1),
        "type_nodes": node_cols(inputs["node_type_119"], 0),
        "wqk": np.ascontiguousarray(np.concatenate([w["Wq"], w["Wk"]], axis=2)),
        "wmT": np.ascontiguousarray(w["Wm"].transpose(0, 2, 1)),
        "wu": w["Wu"],
        "scales": np.ascontiguousarray(np.stack([w[k] for k in ("gq", "gk", "bq", "bk", "go", "bo")], axis=1)),
        "gnbn": np.ascontiguousarray(np.stack([w["gn"], w["bn"]])),
        "f1w": w["F1W"],
        "f1b": w["F1b"].reshape(H, 1),
        "f2": np.ascontiguousarray(np.concatenate([w["F2W"], w["F2b"][None, :]], axis=0)),
        "emb": w["emb"],
        "adapt": w["adapt"],
    }
    for name in ("src", "dst"):
        cols = pad(inputs[name], S, N).reshape(P, T)
        arrays[f"{name}_cols"] = cols
        arrays[f"{name}_rows"] = np.ascontiguousarray(cols.T).reshape(1, S)
    nc = bacc.Bacc("TRN2", target_bir_lowering=False, num_devices=1)
    aps = {k: nc.dram_tensor(f"in_{k}", v.shape, mybir.dt.from_np(v.dtype), kind="ExternalInput").ap()
           for k, v in arrays.items()}
    aps["out"] = nc.dram_tensor("out_0", (N, H), F32, kind="ExternalOutput").ap()
    build(nc, aps)
    r = run(nc, [{f"in_{k}": v for k, v in arrays.items()}], core_ids=[0])
    return r.results[0]["out_0"]
```

```python
from contextlib import ExitStack

import concourse.bass as bass
from concourse import mybir

F32 = mybir.dt.float32
I32 = mybir.dt.int32
BF16 = mybir.dt.bfloat16
ALU = mybir.AluOpType
ACT = mybir.ActivationFunctionType
AX = mybir.AxisListType.X

P = 128
N = 6250
E = 200000
H = 48
RBF = 40
L = 4
GF = 32
NELEM = 119
NB = (N + P) // P
NN = NB * P
T = 1568
S = P * T
TC = 28
PAIRS = T // TC // 2
ROW = 44
C_CW, C_DST, C_SRC = 40, 41, 42
ST = 50
ZROW = S + P
RT = 8
RPAIRS = T // RT // 2
RQ = 4
RLOOPS = T // RT // RQ
HC = 112
OFF = 64
BIG = 1e30
CUT = 6.0
PI = 3.14159265358979


class Chain:

    def __init__(self, eng, sem, base=0):
        self.eng, self.sem, self.base, self.k = eng, sem, base, 0

    def link(self, ins):
        self.k += 1
        ins.then_inc(self.sem, 1)
        self.eng.wait_ge(self.sem, self.base + self.k)

    def last(self, per):
        assert self.k == per, (self.k, per)


def flat(ap):
    return ap.rearrange("p a b -> p (a b)")


def build(nc, a):
    root = ExitStack()
    with root:
        def sb(name, shape, dt=F32, ctx=root):
            return ctx.enter_context(nc.sbuf_tensor(name, shape, dt))

        def sem(name, ctx=root):
            return ctx.enter_context(nc.semaphore(name))

        def cleared(sems):
            with nc.Block() as block:
                @block.gpsimd
                def _(pool):
                    for s in sems:
                        nc.gpsimd.sem_clear(s)

        def two(name, ctx=root):
            return [sem(f"{name}{h}", ctx) for h in range(2)]

        bank = [root.enter_context(nc.psum_tensor(f"bank{i}", [P, 512], F32)) for i in range(8)]

        edges = nc.dram_tensor("edges_by_src", (S, ROW), F32, kind="Internal").ap()
        bydst = nc.dram_tensor("edges_by_dst", (S, 2), I32, kind="Internal").ap()
        fill = nc.dram_tensor("fill_rows", (S + NN, H), F32, kind="Internal").ap()
        state = nc.dram_tensor("state_rows", (S + P + 1, ST), F32, kind="Internal").ap()
        nodes = nc.dram_tensor("node_rows", (NN, 2 * H), F32, kind="Internal").ap()
        elems = nc.dram_tensor("element_rows", (NELEM, 2 * GF), F32, kind="Internal").ap()

        iota_f = sb("iota_f", [P, P])
        pidx = sb("pidx", [P, 1])
        ident = sb("ident", [P, P])
        ident_b = sb("ident_b", [P, P], BF16)
        before = sb("before", [P, P])
        after = sb("after", [P, P])
        ones = sb("ones", [P, P])
        iota_b = sb("iota_b", [P, P], BF16)
        count = [sb(f"count{k}", [P, NB]) for k in range(2)]
        first_i = sb("first_i", [P, NB], I32)
        last_i = [sb(f"last_i{k}", [P, NB], I32) for k in range(2)]

        zero_dma = sem("zero_dma")
        const_chain = sem("const_chain")
        iota_done = sem("iota_done")

        zeros = sb("zeros", [P, TC * H])

        with ExitStack() as ctx:
            iota_i = sb("iota_i", [P, P], I32, ctx)
            pidx_i = sb("pidx_i", [P, 1], I32, ctx)
            block = ctx.enter_context(nc.Block())

            @block.gpsimd
            def _(pool):
                nc.gpsimd.iota(iota_i[:, :], [[1, P]], base=0, channel_multiplier=0).then_inc(iota_done, 1)
                nc.gpsimd.iota(pidx_i[:, :], [[0, 1]], base=0, channel_multiplier=1).then_inc(iota_done, 1)

            @block.vector
            def _(dve):
                c = Chain(dve, const_chain)
                c.link(nc.vector.memset(zeros[:, :], 0.0))
                dve.wait_ge(iota_done, 2)
                c.link(nc.vector.tensor_copy(iota_f[:, :], iota_i[:, :]))
                c.link(nc.vector.tensor_copy(pidx[:, :], pidx_i[:, :]))
                c.link(nc.vector.tensor_copy(iota_b[:, :], iota_f[:, :]))
                c.link(nc.vector.memset(ones[:, :], 1.0))
                for out, op in ((ident, ALU.is_equal), (ident_b, ALU.is_equal), (before, ALU.is_lt),
                                (after, ALU.is_gt)):
                    c.link(nc.vector.tensor_scalar(out[:, :], iota_f[:, :], pidx[:, 0:1], None, op))


        def sort(key):
            tag = "sd"[key]
            keys_in = a["dst_cols" if key else "src_cols"]
            other_in = a["src_cols" if key else "dst_cols"]
            with ExitStack() as sems_ctx, ExitStack() as clear_ctx, ExitStack() as ctx:
                def s_(name, shape, dt=F32):
                    return sb(f"{name}_{tag}", shape, dt, ctx)

                used = []

                def m_(name):
                    used.append(sem(f"{name}_{tag}", sems_ctx))
                    return used[-1]

                def mm_(name, k=2):
                    return [m_(f"{name}{h}") for h in range(k)]

                key_i = s_("key_i", [P, T], I32)
                oth_i = s_("oth_i", [P, T], I32)
                key_f = s_("key_f", [P, T])
                part_i = s_("part_i", [P, T], I32)
                lo_b = s_("lo_b", [P, T + RT], BF16)
                hi_b = s_("hi_b", [P, T + RT], BF16)
                w_all = s_("w_all", [P, T])
                w_tmp = s_("w_tmp", [P, T])
                half_pi = s_("half_pi", [P, 1])
                lo1 = [s_(f"lo1_{h}", [P, RT, P], BF16) for h in range(2)]
                hi1 = [s_(f"hi1_{h}", [P, RT, NB], BF16) for h in range(2)]
                diff = [s_(f"diff_{h}", [P, RT, NB], BF16) for h in range(2)]
                lo1T = [s_(f"lo1T_{h}", [P, RT * P]) for h in range(2)]
                keyrow = [s_(f"keyrow_{h}", [P, RT * P], I32) for h in range(2)]
                seen = s_("seen", [P, NB, RT + 1])
                carry_on = s_("carry_on", [P, NB, RT + 1])
                prod = s_("prod", [P, RT, NB])
                junk = s_("junk", [P, RT, P])
                within = s_("within", [P, RT])
                base = s_("base", [P, RT])
                pos = [s_(f"pos_{q}", [P, RT], I32) for q in range(RQ)]
                rows = [s_(f"rows_{q}", [P, RT, ROW if key == 0 else 2], F32 if key == 0 else I32)
                        for q in range(RQ)]
                tot = s_("tot", [P, NB])
                incl = s_("incl", [P, NB])
                tmp = s_("tmp", [P, NB])
                mask = s_("mask", [P, NB])
                if key == 1:
                    pairs = s_("pairs", [P, T, 2], I32)
                    falls = s_("falls", [P, 1])
                    unsorted_i = s_("unsorted_i", [P, 1], I32)

                clear_ctx.callback(cleared, used)
                loaded, prep, chain = m_("loaded"), m_("prep"), m_("chain")
                hist_in, hist_out = mm_("hist_in"), m_("hist_out")
                hot, hist, prefix = mm_("hot"), mm_("tile_counts"), m_("prefix")
                seen_ok, got = mm_("seen_ok"), mm_("got")
                turned, turned_sb = mm_("turned"), mm_("turned_sb")
                row_dma, key_dma = mm_("row_dma", RQ), mm_("key_dma")
                sent = [sem(f"sent_{tag}{q}") for q in range(RQ)]
                keys_used, pos_ok = mm_("keys_used"), mm_("pos_ok", RQ)
                payload, rows_free = mm_("payload", RQ), mm_("rows_free", RQ)
                go, rank_chain = m_("go"), m_("rank_chain")
                sine, wchain = m_("sine"), m_("wchain")
                next_in, paired, falls_in = m_("next_in"), m_("paired"), m_("falls_in")
                hi_in, diff_ok, squared, hist_go = mm_("hi_in"), mm_("diff_ok"), m_("squared"), m_("hist_go")
                next_free, order_chain = m_("next_free"), m_("order_chain")
                pairs_out = m_("pairs_out")
                tile_counts = [bank[0], bank[1]]
                got_ps = [bank[2], bank[3]]
                turn_ps = [bank[4], bank[5]]
                hist_ps = bank[6]
                tot_ps = bank[7]
                ea_v = a["edge_attr"].rearrange("(p t) f -> p t f", p=P)

                def lo_hot(h, c0):
                    return nc.vector.tensor_tensor(
                        lo1[h][:, :, :], iota_b[:, :].unsqueeze(1).broadcast_to([P, RT, P]),
                        lo_b[:, bass.ds(c0, RT)].unsqueeze(2).broadcast_to([P, RT, P]), ALU.is_equal)

                def one_hot(h, c0):
                    lo_hot(h, c0)
                    nc.vector.tensor_tensor(
                        hi1[h][:, :, :], iota_b[:, 0:NB].unsqueeze(1).broadcast_to([P, RT, NB]),
                        hi_b[:, bass.ds(c0, RT)].unsqueeze(2).broadcast_to([P, RT, NB]), ALU.is_equal
                    ).then_inc(hist_in[h], 1)

                def check_order():
                    with nc.Block() as block:
                        @block.sync
                        def _(sp):
                            sp.dma_start(key_i[:, :], keys_in[:, :]).then_inc(loaded, 16)
                            sp.dma_start(oth_i[:, :], other_in[:, :]).then_inc(loaded, 16)
                            line = keys_in.rearrange("p t -> (p t)")
                            last_row = (P - 1) * T
                            sp.wait_ge(next_free, 1)
                            sp.dma_start(part_i[0:P - 1, :],
                                         line[1:1 + last_row].rearrange("(p t) -> p t", t=T)).then_inc(next_in, 16)
                            sp.dma_start(part_i[P - 1:P, 0:T - 1],
                                         line[1 + last_row:S].rearrange("(p t) -> p t", p=1)).then_inc(next_in, 16)
                            sp.wait_ge(paired, 1)
                            sp.dma_start(bydst.rearrange("(p t) f -> p t f", p=P), pairs[:, :, :]
                                         ).then_inc(pairs_out, 16)
                            sp.wait_ge(pairs_out, 16)

                        @block.scalar
                        def _(act):
                            act.wait_ge(loaded, 32)
                            nc.scalar.copy(pairs[:, :, 0], oth_i[:, :])
                            nc.scalar.copy(pairs[:, :, 1], key_i[:, :]).then_inc(paired, 1)

                        @block.tensor
                        def _(pe):
                            pe.wait_ge(falls_in, 1)
                            nc.tensor.matmul(tile_counts[0][:, 0:1], ones[:, :], falls[:, :], start=True, stop=True
                                             ).then_inc(falls_in, 1)

                        @block.vector
                        def _(dve):
                            c = Chain(dve, order_chain)
                            nc.vector.memset(part_i[:, :], NN).then_inc(next_free, 1)
                            dve.wait_ge(loaded, 32)
                            dve.wait_ge(next_in, 32)
                            c.link(nc.vector.tensor_tensor(w_all[:, :], part_i[:, :], key_i[:, :], ALU.is_lt))
                            nc.vector.tensor_reduce(falls[:, :], w_all[:, :], AX, ALU.add).then_inc(falls_in, 1)
                            dve.wait_ge(falls_in, 2)
                            c.link(nc.vector.tensor_copy(unsorted_i[:, :], tile_counts[0][:, 0:1]))

                def histogram():
                    with nc.Block() as block:
                        histogram_block(block)

                def histogram_block(block):
                    if key == 0:
                        @block.sync
                        def _(sp):
                            sp.dma_start(key_i[:, :], keys_in[:, :]).then_inc(loaded, 16)
                            sp.dma_start(oth_i[:, :], other_in[:, :]).then_inc(loaded, 16)
                            sp.dma_start(w_tmp[:, :], a["edge_weight"][:, :]).then_inc(loaded, 16)
                            fill_v = fill[0:S, :].rearrange("(p t) f -> p (t f)", p=P)
                            with sp.Fori(0, T // TC) as i:
                                sp.dma_start(fill_v[:, bass.ds(i * (TC * H), TC * H)], zeros[:, :]
                                             ).then_inc(zero_dma, 16)
                            sp.dma_start(state[S:S + P, :], zeros[:, 0:ST]).then_inc(zero_dma, 16)
                            sp.dma_start(state[ZROW:ZROW + 1, :], zeros[0:1, 0:ST]).then_inc(zero_dma, 16)
                            sp.wait_ge(zero_dma, 16 * (T // TC + 2))

                        @block.gpsimd
                        def _(pool):
                            with pool.Fori(0, RPAIRS) as i:
                                for h in range(2):
                                    pool.wait_ge(hi_in[h], i + 1)
                                    nc.gpsimd.tensor_tensor(
                                        diff[h][:, :, :], iota_b[:, 0:NB].unsqueeze(1).broadcast_to([P, RT, NB]),
                                        hi_b[:, bass.ds((2 * i + h) * RT, RT)].unsqueeze(2).broadcast_to([P, RT, NB]),
                                        ALU.subtract).then_inc(diff_ok[h], 1)

                        @block.scalar
                        def _(act):
                            act.wait_ge(wchain, 9)
                            nc.scalar.activation(w_all[:, :], w_all[:, :], ACT.Sin, bias=half_pi[:, 0:1],
                                                 scale=-PI / CUT).then_inc(sine, 1)
                            with act.Fori(0, RPAIRS) as i:
                                for h in range(2):
                                    act.wait_ge(diff_ok[h], i + 1)
                                    nc.scalar.activation(diff[h][:, :, :], diff[h][:, :, :], ACT.Square
                                                         ).then_inc(squared, 1)
                                    act.wait_ge(squared, 2 * i + h + 1)
                                    act.wait_ge(hot[h], i + 1)
                                    nc.scalar.activation(hi1[h][:, :, :], diff[h][:, :, :], ACT.Relu,
                                                         bias=ones[:, 0:1], scale=-1.0).then_inc(hi_in[h], 1)

                    else:
                        @block.sync
                        def _(sp):
                            sp.wait_ge(loaded, 32)

                        @block.gpsimd
                        def _(pool):
                            pool.wait_ge(loaded, 32)

                        @block.scalar
                        def _(act):
                            act.wait_ge(loaded, 32)

                    @block.tensor
                    def _(pe):
                        pe.wait_ge(prep, 1)
                        nc.tensor.matmul(hist_ps[:, 0:NB], lo1[0][:, 0, :], hi1[0][:, 0, :], start=True, stop=False,
                                         skip_group_check=True).then_inc(hist_out, 1)
                        with pe.Fori(0, RPAIRS) as i:
                            for h in range(2):
                                pe.wait_ge(hist_in[h], i + 1)
                                if key == 0:
                                    pe.wait_ge(hi_in[h], i + 2)
                                    nc.tensor.sem_inc(hist_go, 1)
                                for j in range(RT):
                                    ins = nc.tensor.matmul(hist_ps[:, 0:NB], lo1[h][:, j, :], hi1[h][:, j, :],
                                                           start=False, stop=False, skip_group_check=True)
                                ins.then_inc(hot[h], 1)
                        pe.wait_ge(prep, 2)
                        nc.tensor.matmul(hist_ps[:, 0:NB], lo1[0][:, 0, :], hi1[0][:, 0, :], start=False, stop=True,
                                         skip_group_check=True).then_inc(hist_out, 1)
                        pe.wait_ge(prep, 3)
                        nc.tensor.matmul(tot_ps[:, 0:NB], ones[:, :], count[key][:, :], start=True, stop=True)
                        nc.tensor.matmul(tot_ps[:, 64:64 + NB], after[:, :], count[key][:, :], start=True,
                                         stop=True).then_inc(prefix, 1)

                    @block.vector
                    def _(dve):
                        c = Chain(dve, chain)
                        w = Chain(dve, wchain)
                        c.link(nc.vector.memset(half_pi[:, :], PI / 2))
                        c.link(nc.vector.memset(lo_b[:, T:T + RT], 0.0))
                        c.link(nc.vector.memset(hi_b[:, T:T + RT], 0.0))
                        c.link(nc.vector.memset(lo1[0][:, 0, :], 0.0))
                        nc.vector.memset(hi1[0][:, 0, :], 0.0).then_inc(prep, 1)
                        dve.wait_ge(prep, 1)
                        if key == 0:
                            dve.wait_ge(loaded, 48)
                            w.link(nc.vector.tensor_single_scalar(w_all[:, :], w_tmp[:, :], 0.5 / CUT, ALU.mult))
                            w.link(nc.vector.tensor_copy(part_i[:, :], w_all[:, :]))
                            w.link(nc.vector.tensor_copy(w_all[:, :], part_i[:, :]))
                            w.link(nc.vector.scalar_tensor_tensor(w_all[:, :], w_all[:, :], -2 * CUT, w_tmp[:, :],
                                                                  ALU.mult, ALU.add))
                            w.link(nc.vector.scalar_tensor_tensor(w_all[:, :], w_all[:, :], -1.0, w_all[:, :],
                                                                  ALU.mult, ALU.max))
                            w.link(nc.vector.tensor_scalar(key_f[:, :], w_all[:, :], -1.0, 2 * CUT, ALU.mult, ALU.add))
                            w.link(nc.vector.tensor_tensor(w_all[:, :], w_all[:, :], key_f[:, :], ALU.min))
                            w.link(nc.vector.tensor_scalar(w_tmp[:, :], w_tmp[:, :], CUT, None, ALU.is_lt))
                            w.link(nc.vector.tensor_scalar(w_all[:, :], w_all[:, :], 0.0, None, ALU.max))
                        c.link(nc.vector.tensor_copy(key_f[:, :], key_i[:, :]))
                        c.link(nc.vector.tensor_single_scalar(part_i[:, :], key_i[:, :], P - 1, ALU.bitwise_and))
                        c.link(nc.vector.tensor_copy(lo_b[:, 0:T], part_i[:, :]))
                        c.link(nc.vector.tensor_single_scalar(part_i[:, :], key_i[:, :], 7, ALU.logical_shift_right))
                        c.link(nc.vector.tensor_copy(hi_b[:, 0:T], part_i[:, :]))
                        dve.wait_ge(hist_out, 1)
                        for h in range(2):
                            nc.vector.sem_inc(hot[h], 1)
                            if key == 0:
                                nc.vector.sem_inc(hi_in[h], 1)
                        with dve.Fori(0, RPAIRS) as i:
                            for h in range(2):
                                dve.wait_ge(hot[h], i + 1)
                                if key == 0:
                                    lo_hot(h, (2 * i + h) * RT).then_inc(hist_in[h], 1)
                                else:
                                    one_hot(h, (2 * i + h) * RT)
                        if key == 0:
                            dve.wait_ge(sine, 1)
                            w.link(nc.vector.tensor_scalar(w_all[:, :], w_all[:, :], 0.5, 0.5, ALU.mult, ALU.add))
                            w.link(nc.vector.tensor_tensor(w_all[:, :], w_all[:, :], w_tmp[:, :], ALU.mult))
                        for h in range(2):
                            dve.wait_ge(hot[h], RPAIRS + 1)
                        c.link(nc.vector.memset(lo1[0][:, 0, :], 0.0))
                        nc.vector.memset(hi1[0][:, 0, :], 0.0).then_inc(prep, 1)
                        dve.wait_ge(hist_out, 2)
                        nc.vector.tensor_copy(count[key][:, :], hist_ps[:, 0:NB]).then_inc(prep, 1)
                        dve.wait_ge(prep, 3)
                        dve.wait_ge(prefix, 1)
                        c.link(nc.vector.tensor_copy(tot[:, :], tot_ps[:, 0:NB]))
                        c.link(nc.vector.tensor_tensor_scan(incl[:, :], ones[:, 0:NB], tot[:, :], 0.0,
                                                            ALU.mult, ALU.add))
                        c.link(nc.vector.tensor_tensor(incl[:, :], incl[:, :], tot[:, :], ALU.subtract))
                        c.link(nc.vector.tensor_tensor(seen[:, :, RT], incl[:, :], tot_ps[:, 64:64 + NB], ALU.add))
                        c.link(nc.vector.tensor_single_scalar(mask[:, :], count[key][:, :], 0.0, ALU.is_gt))
                        c.link(nc.vector.tensor_tensor(tmp[:, :], seen[:, :, RT], count[key][:, :], ALU.add))
                        c.link(nc.vector.tensor_single_scalar(tmp[:, :], tmp[:, :], -1.0 - ZROW, ALU.add))
                        c.link(nc.vector.tensor_tensor(tmp[:, :], tmp[:, :], mask[:, :], ALU.mult))
                        c.link(nc.vector.tensor_single_scalar(tmp[:, :], tmp[:, :], float(ZROW), ALU.add))
                        if key == 0:
                            c.link(nc.vector.tensor_copy(last_i[0][:, :], tmp[:, :]))
                            c.link(nc.vector.tensor_scalar(incl[:, :], iota_f[:, 0:NB], float(P), pidx[:, 0:1],
                                                           ALU.mult, ALU.add))
                            c.link(nc.vector.tensor_single_scalar(incl[:, :], incl[:, :], float(S), ALU.add))
                            c.link(nc.vector.tensor_tensor(tmp[:, :], seen[:, :, RT], incl[:, :], ALU.subtract))
                            c.link(nc.vector.tensor_tensor(tmp[:, :], tmp[:, :], mask[:, :], ALU.mult))
                            c.link(nc.vector.tensor_tensor(tmp[:, :], tmp[:, :], incl[:, :], ALU.add))
                            c.link(nc.vector.tensor_copy(first_i[:, :], tmp[:, :]))

                def rank():
                    with nc.Block() as block:
                        rank_block(block)

                def counts_of(h):
                    return tile_counts[h][:, 0:NB * (RT + 1)].rearrange("p (n j) -> p n j", n=NB)

                def rank_block(block):
                    @block.sync
                    def _(sp):
                        krow = a["dst_rows" if key else "src_rows"]

                        def load(i, q):
                            k = RQ * i + q
                            sp.dma_start(keyrow[q % 2][:, :],
                                         krow[:, bass.ds(k * (RT * P), RT * P)].broadcast_to([P, RT * P])
                                         ).then_inc(key_dma[q % 2], 16)
                            if key == 0:
                                sp.dma_start(rows[q][:, :, 0:RBF], ea_v[:, bass.ds(k * RT, RT), :]
                                             ).then_inc(row_dma[q], 16)

                        for q in range(RQ):
                            nc.sync.sem_inc(rows_free[q], 1)
                            if q >= 2:
                                sp.wait_ge(keys_used[q % 2], q // 2)
                            load(0, q)
                        with sp.Fori(1, RLOOPS) as i:
                            for q in range(RQ):
                                sp.wait_ge(sent[q], 16 * RT * i)
                                nc.sync.sem_inc(rows_free[q], 1)
                                sp.wait_ge(keys_used[q % 2], (RQ // 2) * i + q // 2)
                                load(i, q)
                        for q in range(RQ):
                            sp.wait_ge(sent[q], 16 * RT * RLOOPS)

                    @block.scalar
                    def _(act):
                        with act.Fori(0, RLOOPS) as i:
                            for q in range(RQ):
                                h, n = q % 2, (RQ // 2) * i + q // 2 + 1
                                c0 = (RQ * i + q) * RT
                                act.wait_ge(turned[h], n)
                                nc.scalar.copy(lo1T[h][:, :], bank_bf(turn_ps[h])).then_inc(turned_sb[h], 1)
                                act.wait_ge(rows_free[q], i + 1)
                                if key == 0:
                                    act.wait_ge(row_dma[q], 16 * i + 16)
                                    nc.scalar.copy(rows[q][:, :, C_CW], w_all[:, bass.ds(c0, RT)])
                                    nc.scalar.copy(rows[q][:, :, C_DST].bitcast(I32), oth_i[:, bass.ds(c0, RT)])
                                    nc.scalar.copy(rows[q][:, :, C_SRC + 1], key_f[:, bass.ds(c0, RT)])
                                    nc.scalar.copy(rows[q][:, :, C_SRC].bitcast(I32),
                                                   key_i[:, bass.ds(c0, RT)]).then_inc(payload[q], 1)
                                else:
                                    nc.scalar.copy(rows[q][:, :, 0], oth_i[:, bass.ds(c0, RT)])
                                    nc.scalar.copy(rows[q][:, :, 1], key_i[:, bass.ds(c0, RT)]
                                                   ).then_inc(payload[q], 1)

                    @block.gpsimd
                    def _(pool):
                        out = edges if key == 0 else bydst
                        with pool.Fori(0, RLOOPS) as i:
                            for q in range(RQ):
                                pool.wait_ge(pos_ok[q], i + 1)
                                pool.wait_ge(payload[q], i + 1)
                                nc.gpsimd.sem_inc(go, 1)
                                for j in range(RT):
                                    nc.gpsimd.indirect_dma_start(
                                        out=out[:, :],
                                        out_offset=bass.IndirectOffsetOnAxis(ap=pos[q][:, j:j + 1], axis=0),
                                        in_=rows[q][:, j, :], in_offset=None).then_inc(sent[q], 16)

                    @block.tensor
                    def _(pe):
                        with pe.Fori(0, RLOOPS) as i:
                            for q in range(RQ):
                                h, n = q % 2, (RQ // 2) * i + q // 2 + 1
                                pe.wait_ge(hist_in[h], RPAIRS + n)
                                for j in range(RT):
                                    nc.tensor.transpose(bank_bf(turn_ps[h])[:, j * P:(j + 1) * P], lo1[h][:, j, :],
                                                        ident_b[:, :])
                                nc.tensor.matmul(counts_of(h)[:, :, 1], lo1[h][:, 0, :], hi1[h][:, 0, :],
                                                 start=True, stop=True).then_inc(turned[h], 1)
                                for j in range(1, RT):
                                    ins = nc.tensor.matmul(counts_of(h)[:, :, j + 1], lo1[h][:, j, :],
                                                           hi1[h][:, j, :], start=True, stop=True)
                                ins.then_inc(hist[h], 1)
                                pe.wait_ge(turned_sb[h], n)
                                pe.wait_ge(seen_ok[h], n)
                                for j in range(RT):
                                    ins = nc.tensor.matmul(got_ps[h][:, j * NB:(j + 1) * NB],
                                                           lo1T[h][:, j * P:(j + 1) * P], seen[:, :, j],
                                                           start=True, stop=True)
                                ins.then_inc(got[h], 1)

                    @block.vector
                    def _(dve):
                        one_hot(0, 0)
                        nc.vector.memset(carry_on[:, :, :], 1.0).then_inc(next_free, 1)
                        dve.wait_ge(next_free, 1 + key)
                        nc.vector.memset(carry_on[:, :, 0], 0.0).then_inc(next_free, 1)
                        dve.wait_ge(next_free, 2 + key)
                        per = RQ * (1 + (RT - 1) + 3)
                        with dve.Fori(0, RLOOPS) as i:
                            c = Chain(dve, rank_chain, per * i)
                            for q in range(RQ):
                                h, n = q % 2, (RQ // 2) * i + q // 2 + 1
                                k = RQ * i + q
                                dve.wait_ge(hist[h], n)
                                dve.wait_ge(key_dma[h], 16 * n)
                                c.link(nc.vector.tensor_copy(counts_of(h)[:, :, 0], seen[:, :, RT]))
                                nc.vector.tensor_tensor_scan(
                                    flat(seen[:, :, :]), flat(carry_on[:, :, :]), flat(counts_of(h)), 0.0,
                                    ALU.mult, ALU.add).then_inc(seen_ok[h], 1)
                                for j in range(RT):
                                    nc.vector.scalar_tensor_tensor(
                                        junk[:, j, :], keyrow[h][:, j * P:(j + 1) * P],
                                        key_f[:, bass.ds(k * RT + j, 1)],
                                        before[:, :], ALU.is_equal, ALU.mult, accum_out=within[:, j:j + 1]
                                    ).then_inc(keys_used[h] if j == RT - 1 else rank_chain, 1)
                                c.k += RT - 1
                                dve.wait_ge(rank_chain, c.base + c.k)
                                dve.wait_ge(seen_ok[h], n)
                                dve.wait_ge(keys_used[h], n)
                                one_hot(1 - h, (k + 1) * RT)
                                dve.wait_ge(got[h], n)
                                c.link(nc.vector.tensor_tensor(
                                    prod[:, :, :], got_ps[h][:, 0:RT * NB].rearrange("p (j n) -> p j n", j=RT),
                                    hi1[h][:, :, :], ALU.mult))
                                c.link(nc.vector.tensor_reduce(base[:, :], prod[:, :, :], AX, ALU.add))
                                c.link(nc.vector.tensor_tensor(base[:, :], base[:, :], within[:, :], ALU.add))
                                dve.wait_ge(rows_free[q], i + 1)
                                nc.vector.tensor_copy(pos[q][:, :], base[:, :]).then_inc(pos_ok[q], 1)
                            c.last(per)

                if key == 0:
                    histogram()
                    rank()
                else:
                    check_order()
                    with nc.If(nc.values_load(unsorted_i[0:1, 0:1], min_val=0, max_val=S) > 0):
                        histogram()
                        rank()

        def bank_bf(b):
            return b[:, :].bitcast(BF16)

        sort(0)
        sort(1)
        passes(nc, a, root, sb, sem, two, bank, (edges, bydst, fill, state, nodes, elems),
               (iota_f, iota_b, pidx, ident, ones, after, count, first_i, last_i))


GATE_BANK = 10


def pass_sems(two, sem):
    names = ("row_landed", "fill_landed", "so_stored", "rows_used", "g_used", "qi_ready",
             "prod_done", "s_ready", "coef_ready", "v_done", "so_ready", "flags_ready", "cf_ready")
    d = {n: two(n) for n in names}
    for kind in ("init", "layer", "nbr"):
        d["g_landed", kind] = two(f"g_landed_{kind}")
        d["chain", kind] = sem(f"pass_chain_{kind}")
    return d


def passes(nc, a, root, sb, sem, two, bank, tabs, cst):
    edges, bydst, fill, state, nodes, elems = tabs
    iota_f, iota_b, pidx, ident, ones, after, count, first_i, last_i = cst
    qnodes = nc.dram_tensor("source_rows", (NN, H), F32, kind="Internal").ap()

    srcf = sb("srcf", [P, T])
    same = sb("same", [P, T])
    logm = sb("logm", [P, T])
    hc = sb("hc", [P, NB, HC])
    GW = 2 * TC * 2 * H
    arena = sb("arena", [P, 2 * GW])
    g_all = arena[:, 0:GW].rearrange("p (a t f) -> p a t f", a=2, t=TC)
    pf_all = arena[:, GW:2 * GW].rearrange("p (a f) -> p a f", a=4)
    x2 = arena[:, 0:GW]
    sq_all = arena[:, GW:2 * GW]
    ns = sb("ns", [P, NB, ST])
    ea = [sb(f"ea{h}", [P, TC, ROW]) for h in range(2)]
    pair_i = [sb(f"pair_i{h}", [P, TC, 2], I32) for h in range(2)]
    qi = [sb(f"qi{h}", [P, H, TC + 1]) for h in range(2)]
    cf = [sb(f"cf{h}", [P, H + 1, TC + 1]) for h in range(2)]
    ce = [sb(f"ce{h}", [P, H + 1, TC + 1]) for h in range(2)]
    v = [sb(f"v{h}", [P, H + 1, TC + 1]) for h in range(2)]
    so = [sb(f"so{h}", [P, TC, ST]) for h in range(2)]
    sc = [sb(f"sc{h}", [P, TC]) for h in range(2)]
    mx = [sb(f"mx{h}", [P, TC + 1]) for h in range(2)]
    k1 = [sb(f"k1{h}", [P, TC + 1]) for h in range(2)]
    d1 = [sb(f"d1{h}", [P, TC]) for h in range(2)]
    d2 = [sb(f"d2{h}", [P, TC]) for h in range(2)]
    es = [sb(f"es{h}", [P, TC]) for h in range(2)]
    pen = sb("pen", [P, TC])
    qc = sb("qc", [P, H])
    vc = sb("vc", [P, H + 1])
    mc = sb("mc", [P, 1])
    kc = sb("kc", [P, 1])
    first_key = sb("first_key", [P, 1], I32)
    prevf = sb("prevf", [P, 1])
    lastf = sb("lastf", [P, 1])
    cont = sb("cont", [P, 1])
    nrun = sb("nrun", [P, 1])
    fix_f = sb("fix_f", [P, 1])
    fix_i = sb("fix_i", [P, 1], I32)
    diag = sb("diag", [P, P])
    chb = sb("chb", [H + 1, P])
    penc = sb("penc", [H + 1, P])
    mr = sb("mr", [H + 1, P])
    mcar = sb("mcar", [H + 1, P + 1])
    arg = sb("arg", [H + 1, 2 * P])
    vcar = sb("vcar", [H + 1, P + 1])
    fx = sb("fx", [P, ST])
    fm = sb("fm", [P, 1])
    fa = sb("fa", [P, 2])
    stat = sb("stat", [P, 2 * NB])
    ht1 = sb("ht1", [HC, NB // 7 * P])
    ht2 = sb("ht2", [H, NB // 7 * P])
    wqk = sb("wqk", [H, 2 * H])
    wu = sb("wu", [HC, H])
    wub = sb("wub", [H, H])
    wmT = sb("wmT", [H, H])
    gb = sb("gb", [P, 4, H])
    gn = sb("gn", [P, 2, H])
    f1w = sb("f1w", [RBF, H])
    f1b = sb("f1b", [H, 1])
    f2 = sb("f2", [H + 1, H])
    eaT = [sb(f"eaT{h}", [RBF, 4 * P]) for h in range(2)]
    hid = [sb(f"hid{h}", [64, 4 * P]) for h in range(2)]
    dis = sb("dis", [P, NB])

    PS = pass_sems(two, sem)
    xv48 = x2[:, 0:NB * H].rearrange("p (n f) -> p n f", f=H)
    sem_rows = sem("setup_dma")
    setup_chain = sem("setup_chain")
    kc_ready, kc_dma = sem("kc_ready"), sem("kc_dma")
    emb_ps = sem("emb_ps")
    emb_sb = sem("emb_sb")
    ee_dma = sem("ee_dma")
    ee_rows = sem("ee_rows")
    go, pe_go = sem("pool_go"), sem("pe_go")

    HALF = TC // 2
    dst_parts = ns[:, :, :].rearrange("p n f -> p (n f)")[:, 0:T].bitcast(BF16)
    dst_lo, dst_hi = dst_parts[:, 0:T], dst_parts[:, T:2 * T]
    hot_rows = [flat(ce[e][:, :, :]).bitcast(BF16) for e in range(2)]
    dst_lo1 = [r[:, 0:HALF * P].rearrange("p (t f) -> p t f", f=P) for r in hot_rows]
    dst_hi1 = [r[:, HALF * P:HALF * (P + NB)].rearrange("p (t f) -> p t f", f=NB) for r in hot_rows]
    dst_hot, dst_used, dst_done = two("dst_hot"), two("dst_used"), sem("dst_done")

    def root_site(name):
        return sem(f"var_{name}"), sem(f"std_{name}")

    qn = xv48
    nrow = sq_all[:, 0:NB * 2 * H].rearrange("p (n f) -> p n f", f=2 * H)
    dst_int, dst_bits = logm[:, :].bitcast(I32), same[:, :].bitcast(I32)
    with ExitStack() as ctx:
        emb = sb("emb", [P, GF], F32, ctx)
        embT = sb("embT", [GF, P], F32, ctx)
        adapt = sb("adapt", [GF, GF], F32, ctx)
        ee = sb("ee", [P, 2 * GF], F32, ctx)
        typ = sb("typ", [P, NB], I32, ctx)
        mul = sb("mul", [P, NB], F32, ctx)
        eg = sb("eg", [P, NB, 2 * GF], F32, ctx)
        block = ctx.enter_context(nc.Block())

        @block.sync
        def _(sp):
            sp.dma_start(emb[0:NELEM, :], a["emb"]).then_inc(sem_rows, 16)
            sp.dma_start(adapt[:, :], a["adapt"]).then_inc(sem_rows, 16)
            sp.dma_start(typ[:, :], a["type_nodes"]).then_inc(sem_rows, 16)
            sp.dma_start(mul[:, :], a["mult_nodes"]).then_inc(sem_rows, 16)
            sp.dma_start(hc[:, :, 0:H], a["x_nodes"]).then_inc(sem_rows, 16)
            sp.dma_start(dst_int[:, :], a["dst_cols"][:, :]).then_inc(sem_rows, 16)
            sp.dma_start(f1w[:, :], a["f1w"]).then_inc(sem_rows, 16)
            sp.dma_start(f1b[:, :], a["f1b"]).then_inc(sem_rows, 16)
            sp.dma_start(f2[:, :], a["f2"]).then_inc(sem_rows, 16)
            sp.dma_start(gn[:, :, :], a["gnbn"].rearrange("(o a) f -> o a f", o=1).broadcast_to([P, 2, H])
                         ).then_inc(sem_rows, 16)
            sp.dma_start(first_key[:, :], edges.rearrange("(p t) f -> p t f", p=P)[:, 0, C_SRC:C_SRC + 1].bitcast(I32),
                         allow_slow_non_contiguous=True).then_inc(sem_rows, 16)
            sp.wait_ge(kc_ready, 1)
            sp.dma_start(kc[1:P, :], edges.rearrange("(p t) f -> p t f", p=P)[0:P - 1, T - 1, C_SRC + 1:C_SRC + 2],
                         allow_slow_non_contiguous=True).then_inc(kc_dma, 16)
            sp.wait_ge(kc_dma, 16)
            sp.wait_ge(emb_sb, 2)
            sp.dma_start(elems, ee[0:NELEM, :]).then_inc(ee_dma, 16)
            sp.wait_ge(ee_dma, 16)

        @block.tensor
        def _(pe):
            pe.wait_ge(sem_rows, 176)
            nc.tensor.transpose(bank[0][0:GF, 0:NELEM], emb[0:NELEM, :], ident[0:NELEM, 0:NELEM]).then_inc(emb_ps, 1)
            pe.wait_ge(emb_sb, 1)
            nc.tensor.matmul(bank[1][0:NELEM, 0:GF], embT[:, 0:NELEM], adapt[:, :], start=True, stop=True
                             ).then_inc(emb_ps, 1)

        @block.gpsimd
        def _(pool):
            pool.wait_ge(ee_dma, 16)
            for j in range(NB):
                nc.gpsimd.indirect_dma_start(out=eg[:, j, :], out_offset=None, in_=elems,
                                             in_offset=bass.IndirectOffsetOnAxis(ap=typ[:, j:j + 1], axis=0)
                                             ).then_inc(ee_rows, 16)

        @block.vector
        def _(dve):
            c = Chain(dve, setup_chain)
            for h in range(2):
                for name in ("rows_used", "g_used", "qi_ready", "prod_done", "so_ready"):
                    nc.vector.sem_inc(PS[name][h], 1)
            for h in range(2):
                c.link(nc.vector.memset(cf[h][:, :, 0], 0.0))
                c.link(nc.vector.memset(ce[h][:, :, :], 0.0))
                c.link(nc.vector.memset(so[h][:, :, :], 0.0))
            for h in range(2):
                c.link(nc.vector.memset(hid[h][:, :], 1.0))
            c.link(nc.vector.memset(wu[:, :], 0.0))
            c.link(nc.vector.memset(hc[:, :, H:HC], 0.0))
            c.link(nc.vector.memset(qn[:, :, :], 0.0))
            c.link(nc.vector.memset(nrow[:, :, :], 0.0))
            for tile, value in ((vc, 0.0), (mc, 0.0), (kc, -1.0), (prevf, -1.0)):
                c.link(nc.vector.memset(tile[:, :], value))
            nc.vector.sem_inc(kc_ready, 1)
            dve.wait_ge(sem_rows, 176)
            c.link(nc.vector.tensor_copy(ee[0:NELEM, 0:GF], emb[0:NELEM, :]))
            dve.wait_ge(emb_ps, 1)
            nc.vector.tensor_copy(embT[:, 0:NELEM], bank[0][0:GF, 0:NELEM]).then_inc(emb_sb, 1)
            dve.wait_ge(emb_ps, 2)
            nc.vector.tensor_copy(ee[0:NELEM, GF:2 * GF], bank[1][0:NELEM, 0:GF]).then_inc(emb_sb, 1)
            c.link(nc.vector.tensor_copy(nrow[:, :, GF], mul[:, :]))
            c.link(nc.vector.tensor_copy(nrow[:, :, H:2 * H], hc[:, :, 0:H]))
            for out, op, bits in ((dst_lo, ALU.bitwise_and, P - 1), (dst_hi, ALU.logical_shift_right, 7)):
                c.link(nc.vector.tensor_single_scalar(dst_bits, dst_int, bits, op))
                c.link(nc.vector.tensor_copy(out, dst_bits))
            dve.wait_ge(ee_rows, 16 * NB)
            c.link(nc.vector.tensor_copy(qn[:, :, 0:GF], eg[:, :, 0:GF]))
            c.link(nc.vector.tensor_copy(nrow[:, :, 0:GF], eg[:, :, GF:2 * GF]))

    def publish(tag, run, src_rows, parts, sems):
        table, scattered, began = sems
        node_v = nodes.rearrange("(n p) f -> p n f", p=P)
        q_v = qnodes.rearrange("(n p) f -> p n f", p=P)
        n_dma = len(parts) + 1
        with ExitStack() as ctx:
            block = ctx.enter_context(nc.Block())

            @block.sync
            def _(sp):
                for cols, values in parts:
                    sp.dma_start(node_v[:, :, cols], values).then_inc(table, 16)
                sp.dma_start(q_v, src_rows).then_inc(table, 16)
                sp.wait_ge(began, 16)
                sp.wait_ge(scattered, 16 * NB)

            @block.gpsimd
            def _(pool):
                for j in range(NB):
                    nc.gpsimd.indirect_dma_start(
                        out=fill, out_offset=bass.IndirectOffsetOnAxis(ap=first_i[:, j:j + 1], axis=0),
                        in_=src_rows[:, j, :], in_offset=None).then_inc(scattered, 16)
                pool.wait_ge(table, 16 * n_dma * run + 16 * n_dma)
                nc.gpsimd.sem_inc(go, 1)
                nc.gpsimd.indirect_dma_start(
                    out=qc[:, :], out_offset=None, in_=qnodes,
                    in_offset=bass.IndirectOffsetOnAxis(ap=first_key[:, 0:1], axis=0)).then_inc(began, 16)

    def publish_sems(kind):
        return [sem(f"{n}_{kind}") for n in ("table", "scattered", "began")]

    publish("init", 0, qn, ((slice(0, 2 * H), nrow),), publish_sems("init"))

    def edge_pass(kind, run):
        m = PS
        done = {"init": 0, "layer": run + 1, "nbr": L + 1}[kind]
        keyed_done = {"init": 0, "layer": 0, "nbr": 1}[kind]
        rows_v = (bydst if kind == "nbr" else edges).rearrange("(p t) f -> p t f", p=P)
        fill_v = fill[0:S, :].rearrange("(p t) f -> p (t f)", p=P)
        state_v = state[0:S, :].rearrange("(p t) f -> p t f", p=P)
        keyed = kind in ("init", "nbr")
        rbuf = pair_i if kind == "nbr" else ea
        with ExitStack() as ctx:
            block = ctx.enter_context(nc.Block())

            @block.sync
            def _(sp):
                with sp.Fori(0, PAIRS) as i:
                    for h in range(2):
                        n = done * PAIRS + i + 1
                        k = 2 * i + h
                        sp.wait_ge(m["rows_used"][h], n)
                        sp.dma_start(rbuf[h][:, :, :], rows_v[:, bass.ds(k * TC, TC), :]
                                     ).then_inc(m["row_landed"][h], 16)
                        if kind != "nbr":
                            sp.wait_ge(m["qi_ready"][h], n)
                            sp.dma_start(pf_all[:, 2 + h, :], fill_v[:, bass.ds(k * (TC * H), TC * H)]
                                         ).then_inc(m["fill_landed"][h], 16)

            @block.gpsimd
            def _(pool):
                with pool.Fori(0, PAIRS) as i:
                    for h in range(2):
                        n = done * PAIRS + i + 1
                        pool.wait_ge(m["row_landed"][h], 16 * n)
                        pool.wait_ge(m["g_used"][h], n)
                        nc.gpsimd.sem_inc(go, 1)
                        for t in range(TC):
                            if kind == "nbr":
                                idx, src, out = pair_i[h][:, t, 0:1], qnodes, g_all[:, h, t, 0:H]
                            else:
                                idx = ea[h][:, t, C_DST:C_DST + 1].bitcast(I32)
                                src, out = nodes, g_all[:, h, t, :]
                            nc.gpsimd.indirect_dma_start(
                                out=out, out_offset=None, in_=src,
                                in_offset=bass.IndirectOffsetOnAxis(ap=idx, axis=0)
                            ).then_inc(m["g_landed", kind][h], 16)

            @block.scalar
            def _(act):
                def gates(i, h):
                    k = 2 * i + h

                    def attributes(q):
                        act.wait_ge(et_ready, GQ * k + q + 1)
                        nc.scalar.copy(eaT[q % 2][:, :], bank[q % 2][0:RBF, :]).then_inc(eat_ready, 1)

                    attributes(0)
                    attributes(1)
                    for q in range(GQ):
                        act.wait_ge(hp_ready, GQ * k + q + 1)
                        nc.scalar.activation(hid[q % 2][0:H, :], hid_ps[q % 2][0:H, :], ACT.Silu, bias=f1b[:, 0:1]
                                             ).then_inc(hid_ready, 1)
                        if q + 2 < GQ:
                            attributes(q + 2)
                    act.wait_ge(m["g_used"][h], i + 1)
                    act.wait_ge(gate_ready, k + 1)
                    prod = pf_all[:, h, :]
                    for b in range(-(-TC // GATE_BANK)):
                        t0, t1 = b * GATE_BANK, min(TC, (b + 1) * GATE_BANK)
                        ins = nc.scalar.copy(prod[:, t0 * H:t1 * H], bank[3 + b][:, 0:(t1 - t0) * H])
                    ins.then_inc(gate_read, 1)

                def spread(i, h):
                    n = done * PAIRS + i + 1
                    k = 2 * i + h
                    act.wait_ge(m["prod_done"][h], n)
                    if keyed:
                        act.wait_ge(m["flags_ready"][h], keyed_done * PAIRS + i + 1)
                    nc.scalar.copy(cf[h][:, :, 1:TC + 1],
                                   same[:, bass.ds(k * TC, TC)].unsqueeze(1).broadcast_to([P, H + 1, TC])
                                   ).then_inc(m["cf_ready"][h], 1)
                    if kind != "nbr":
                        act.wait_ge(m["fill_landed"][h], 16 * n)
                        nc.scalar.copy(qi[h][:, :, 1:TC + 1],
                                       pf_all[:, 2 + h, :].rearrange("p (t f) -> p f t", f=H)
                                       ).then_inc(m["qi_ready"][h], 1)

                def exponentials(i, h):
                    act.wait_ge(m["s_ready"][h], run * PAIRS + i + 1)
                    nc.scalar.activation(es[h][:, :], d2[h][:, :], ACT.Exp)
                    nc.scalar.activation(ce[h][:, :, 1:TC + 1],
                                         d1[h][:, :].unsqueeze(1).broadcast_to([P, H + 1, TC]), ACT.Exp
                                         ).then_inc(m["coef_ready"][h], 1)

                def store(i, h):
                    n = done * PAIRS + i + 1
                    act.wait_ge(m["v_done"][h], n)
                    w = H if kind == "nbr" else H + 1
                    if kind == "layer":
                        nc.scalar.copy(so[h][:, :, H + 1], mx[h][:, 1:TC + 1])
                    nc.scalar.copy(so[h][:, :, 0:w].rearrange("p t f -> p f t"), v[h][:, 0:w, 1:TC + 1]
                                   ).then_inc(m["so_ready"][h], 1)
                    act.wait_ge(m["so_ready"][h], n + 1)
                    act.dma_start(state_v[:, bass.ds((2 * i + h) * TC, TC), :], so[h][:, :, :]
                                  ).then_inc(m["so_stored"][h], 16)

                def stored(i):
                    for h in range(2):
                        act.wait_ge(m["so_stored"][h], 16 * (done * PAIRS + i + 1))

                if kind == "init":
                    gates(0, 0)
                    spread(0, 0)
                    with act.Fori(0, PAIRS - 1) as i:
                        gates(i, 1)
                        store(i, 0)
                        spread(i, 1)
                        gates(i + 1, 0)
                        store(i, 1)
                        spread(i + 1, 0)
                        stored(i)
                    gates(PAIRS - 1, 1)
                    store(PAIRS - 1, 0)
                    spread(PAIRS - 1, 1)
                    store(PAIRS - 1, 1)
                    stored(PAIRS - 1)
                else:
                    with act.Fori(0, PAIRS) as i:
                        for h in range(2):
                            spread(i, h)
                            if kind == "layer":
                                exponentials(i, h)
                            store(i, h)
                        stored(i)

            if kind == "init":
                @block.tensor
                def _(pe):
                    nc.tensor.matmul(bank[6][:, 0:NB], dst_lo1[0][:, 0, :], dst_hi1[0][:, 0, :], start=True,
                                     stop=False, skip_group_check=True).then_inc(dst_done, 1)
                    with pe.Fori(0, PAIRS) as i:
                        for h in range(2):
                            pe.wait_ge(m["row_landed"][h], 16 * i + 16)
                            nc.tensor.sem_inc(pe_go, 1)

                            def attributes(q):
                                for j in range(4):
                                    ins = nc.tensor.transpose(bank[q % 2][0:RBF, j * P:(j + 1) * P],
                                                              ea[h][:, 4 * q + j, 0:RBF], ident[:, :])
                                ins.then_inc(et_ready, 1)

                            def hidden(q):
                                pe.wait_ge(eat_ready, (2 * GQ) * i + GQ * h + q + 1)
                                nc.tensor.sem_inc(pe_go, 1)
                                nc.tensor.matmul(hid_ps[q % 2][0:H, :], f1w[:, :], eaT[q % 2][:, :], start=True,
                                                 stop=True).then_inc(hp_ready, 1)

                            attributes(0)
                            attributes(1)
                            hidden(0)
                            for q in range(GQ):
                                if q + 1 < GQ:
                                    hidden(q + 1)
                                if q + 2 < GQ:
                                    attributes(q + 2)
                                pe.wait_ge(hid_ready, (2 * GQ) * i + GQ * h + q + 1)
                                nc.tensor.sem_inc(pe_go, 1)
                                if q == 0:
                                    pe.wait_ge(gate_read, 2 * i + h + 1)
                                    nc.tensor.sem_inc(pe_go, 1)
                                for j in range(4):
                                    t = 4 * q + j
                                    o = (t % GATE_BANK) * H
                                    ins = nc.tensor.matmul(bank[3 + t // GATE_BANK][:, o:o + H],
                                                           hid[q % 2][0:H + 1, j * P:(j + 1) * P], f2[:, :],
                                                           start=True, stop=True)
                                if q == GQ - 1:
                                    ins.then_inc(gate_ready, 1)
                            for e in range(2):
                                pe.wait_ge(dst_hot[e], 2 * i + h + 1)
                                nc.tensor.sem_inc(pe_go, 1)
                                for j in range(HALF):
                                    ins = nc.tensor.matmul(bank[6][:, 0:NB], dst_lo1[e][:, j, :],
                                                           dst_hi1[e][:, j, :], start=False, stop=False,
                                                           skip_group_check=True)
                                ins.then_inc(dst_used[e], 1)
                    pe.wait_ge(dst_done, 2)
                    nc.tensor.matmul(bank[6][:, 0:NB], dst_lo1[0][:, 0, :], dst_hi1[0][:, 0, :], start=False,
                                     stop=True, skip_group_check=True).then_inc(dst_done, 1)

            @block.vector
            def _(dve):
                if kind == "init":
                    nc.vector.sem_inc(gate_read, 1)
                    dve.wait_ge(dst_done, 1)
                    for e in range(2):
                        nc.vector.sem_inc(dst_used[e], 1)
                per = {"init": 22, "layer": 30, "nbr": 4}[kind]
                with dve.Fori(0, PAIRS) as i:
                    c = Chain(dve, m["chain", kind], (run * PAIRS + i) * per)
                    for h in range(2):
                        n = done * PAIRS + i + 1
                        k = 2 * i + h
                        gh = g_all[:, h, :, :]
                        prod = pf_all[:, h, :].rearrange("p (t f) -> p t f", f=H)
                        dve.wait_ge(m["row_landed"][h], 16 * n)
                        if keyed:
                            keys = pair_i[h][:, :, 1] if kind == "nbr" else ea[h][:, :, C_SRC + 1]
                            nc.vector.tensor_copy(srcf[:, bass.ds(k * TC, TC)], keys)
                            nc.vector.tensor_copy(k1[h][:, 0:1], kc[:, :])
                            c.link(nc.vector.tensor_copy(k1[h][:, 1:TC + 1], keys))
                            nc.vector.tensor_copy(kc[:, :], k1[h][:, TC:TC + 1])
                            nc.vector.tensor_tensor(same[:, bass.ds(k * TC, TC)], k1[h][:, 1:TC + 1],
                                                    k1[h][:, 0:TC], ALU.is_equal).then_inc(m["flags_ready"][h], 1)
                        if kind == "layer":
                            dve.wait_ge(m["g_landed", kind][h], 16 * TC * (run * PAIRS + i + 1))
                            nc.vector.scalar_tensor_tensor(gh[:, :, 0:RBF], ea[h][:, :, 0:RBF], 0.1,
                                                           gh[:, :, 0:RBF], ALU.mult, ALU.add
                                                           ).then_inc(m["rows_used"][h], 1)
                        if kind == "init":
                            for e in range(2):
                                dve.wait_ge(dst_used[e], 2 * i + h + 1)
                                t0 = k * TC + e * HALF
                                nc.vector.tensor_tensor(
                                    dst_lo1[e], iota_b[:, :].unsqueeze(1).broadcast_to([P, HALF, P]),
                                    dst_lo[:, bass.ds(t0, HALF)].unsqueeze(2).broadcast_to([P, HALF, P]),
                                    ALU.is_equal)
                                nc.vector.tensor_tensor(
                                    dst_hi1[e], iota_b[:, 0:NB].unsqueeze(1).broadcast_to([P, HALF, NB]),
                                    dst_hi[:, bass.ds(t0, HALF)].unsqueeze(2).broadcast_to([P, HALF, NB]),
                                    ALU.is_equal).then_inc(dst_hot[e], 1)
                        if kind != "nbr":
                            dve.wait_ge(m["qi_ready"][h], n + 1)
                            dve.wait_ge(m["cf_ready"][h], n)
                            c.link(nc.vector.tensor_copy(qi[h][:, :, 0], qc[:, :]))
                            c.link(nc.vector.tensor_tensor_scan(flat(qi[h][:, :, :]), flat(cf[h][:, 0:H, :]),
                                                                flat(qi[h][:, :, :]), 0.0, ALU.mult, ALU.add))
                            c.link(nc.vector.tensor_copy(qc[:, :], qi[h][:, :, TC]))
                        if kind == "layer":
                            dve.wait_ge(m["rows_used"][h], n + 1)
                            c.link(nc.vector.tensor_tensor(
                                prod, qi[h][:, :, 1:TC + 1].rearrange("p f t -> p t f"), gh[:, :, 0:H], ALU.mult))
                            nc.vector.tensor_reduce(sc[h][:, :], prod, AX, ALU.add).then_inc(m["prod_done"][h], 1)
                            dve.wait_ge(m["prod_done"][h], n + 1)
                            c.link(nc.vector.tensor_tensor(sc[h][:, :], sc[h][:, :],
                                                           logm[:, bass.ds(k * TC, TC)], ALU.add))
                            c.link(nc.vector.tensor_scalar(pen[:, :], same[:, bass.ds(k * TC, TC)], BIG, -BIG,
                                                           ALU.mult, ALU.add))
                            dve.wait_ge(m["so_ready"][h], n)
                            c.link(nc.vector.tensor_copy(mx[h][:, 0:1], mc[:, :]))
                            c.link(nc.vector.tensor_tensor_scan(mx[h][:, 1:TC + 1], pen[:, :], sc[h][:, :],
                                                                mx[h][:, 0:1], ALU.add, ALU.max))
                            c.link(nc.vector.tensor_copy(mc[:, :], mx[h][:, TC:TC + 1]))
                            c.link(nc.vector.tensor_tensor(d1[h][:, :], mx[h][:, 0:TC], mx[h][:, 1:TC + 1],
                                                           ALU.subtract))
                            c.link(nc.vector.scalar_tensor_tensor(d1[h][:, :], d1[h][:, :], 0.0, pen[:, :],
                                                                  ALU.min, ALU.add))
                            c.link(nc.vector.tensor_tensor(d2[h][:, :], sc[h][:, :], mx[h][:, 1:TC + 1],
                                                           ALU.subtract))
                            nc.vector.tensor_single_scalar(d2[h][:, :], d2[h][:, :], 20.0, ALU.min
                                                           ).then_inc(m["s_ready"][h], 1)
                            dve.wait_ge(m["coef_ready"][h], run * PAIRS + i + 1)
                            c.link(nc.vector.tensor_copy(v[h][:, H, 1:TC + 1], es[h][:, :]))
                            nc.vector.tensor_tensor(
                                v[h][:, 0:H, 1:TC + 1], gh[:, :, H:2 * H].rearrange("p t f -> p f t"),
                                es[h][:, :].unsqueeze(1).broadcast_to([P, H, TC]), ALU.mult
                            ).then_inc(m["g_used"][h], 1)
                            coef = ce
                        elif kind == "init":
                            dve.wait_ge(m["g_landed", kind][h], 16 * TC * (run * PAIRS + i + 1))
                            c.link(nc.vector.tensor_tensor(
                                gh[:, :, 0:GF], qi[h][:, 0:GF, 1:TC + 1].rearrange("p f t -> p t f"),
                                gh[:, :, 0:GF], ALU.mult))
                            c.link(nc.vector.tensor_reduce(sc[h][:, :], gh[:, :, 0:GF], AX, ALU.add))
                            c.link(nc.vector.tensor_copy(logm[:, bass.ds(k * TC, TC)], gh[:, :, GF]))
                            dve.wait_ge(gate_read, 2 * i + h + 2)
                            nc.vector.tensor_tensor(es[h][:, :], ea[h][:, :, C_CW], gh[:, :, GF], ALU.mult
                                                    ).then_inc(m["rows_used"][h], 1)
                            c.link(nc.vector.tensor_tensor(
                                prod, prod, sc[h][:, :].unsqueeze(2).broadcast_to([P, TC, H]), ALU.add))
                            c.link(nc.vector.tensor_tensor(prod, prod, gh[:, :, H:2 * H], ALU.mult))
                            dve.wait_ge(m["so_ready"][h], n)
                            c.link(nc.vector.tensor_copy(v[h][:, H, 1:TC + 1], gh[:, :, GF]))
                            nc.vector.tensor_tensor(
                                v[h][:, 0:H, 1:TC + 1], prod.rearrange("p t f -> p f t"),
                                es[h][:, :].unsqueeze(1).broadcast_to([P, H, TC]), ALU.mult
                            ).then_inc(m["g_used"][h], 1)
                            coef = cf
                        else:
                            dve.wait_ge(m["g_landed", kind][h], 16 * TC * (run * PAIRS + i + 1))
                            dve.wait_ge(m["so_ready"][h], n)
                            dve.wait_ge(m["flags_ready"][h], keyed_done * PAIRS + i + 1)
                            nc.vector.tensor_copy(v[h][:, 0:H, 1:TC + 1],
                                                  gh[:, :, 0:H].rearrange("p t f -> p f t")
                                                  ).then_inc(m["g_used"][h], 1)
                            dve.wait_ge(m["cf_ready"][h], n)
                            nc.vector.sem_inc(m["rows_used"][h], 1)
                            coef = cf
                        w = H if kind == "nbr" else H + 1
                        c.link(nc.vector.tensor_copy(v[h][:, 0:w, 0], vc[:, 0:w]))
                        dve.wait_ge(m["g_used"][h], n + 1)
                        nc.vector.tensor_tensor_scan(flat(v[h][:, 0:w, :]), flat(coef[h][:, 0:w, :]),
                                                     flat(v[h][:, 0:w, :]), 0.0, ALU.mult, ALU.add
                                                     ).then_inc(m["v_done"][h], 1)
                        dve.wait_ge(m["v_done"][h], n)
                        if keyed:
                            nc.vector.tensor_copy(vc[:, 0:w], v[h][:, 0:w, TC]).then_inc(m["prod_done"][h], 1)
                            dve.wait_ge(m["prod_done"][h], n + 1)
                        else:
                            c.link(nc.vector.tensor_copy(vc[:, 0:w], v[h][:, 0:w, TC]))
                    c.last(per)
                if kind == "init":
                    for e in range(2):
                        dve.wait_ge(dst_used[e], 2 * PAIRS + 1)
                    nc.vector.memset(dst_hi1[0][:, 0, :], 0.0).then_inc(dst_done, 1)

    GQ = TC // 4
    hid_ps = (bank[2], bank[7])
    et_ready, eat_ready, hp_ready = sem("et_ready"), sem("eat_ready"), sem("hp_ready")
    hid_ready, gate_ready, gate_read = sem("hid_ready"), sem("gate_ready"), sem("gate_read")

    def crossings(tag):
        with ExitStack() as ctx:
            chain, shifted, wanted, turned = (sem(f"{n}_{tag}") for n in
                                              ("cross_chain", "shifted", "last_ready", "cross_ps"))
            block = ctx.enter_context(nc.Block())

            @block.sync
            def _(sp):
                sp.wait_ge(wanted, 1)
                sp.dma_start(prevf[1:P, :], lastf[0:P - 1, :]).then_inc(shifted, 16)
                sp.wait_ge(shifted, 16)

            @block.tensor
            def _(pe):
                if tag == "init":
                    pe.wait_ge(dst_done, 4)
                    nc.tensor.matmul(bank[1][:, 0:NB], ones[:, :], count[1][:, :], start=True, stop=True)
                    nc.tensor.matmul(bank[2][:, 0:NB], after[:, :], count[1][:, :], start=True, stop=True
                                     ).then_inc(dst_done, 1)
                pe.wait_ge(wanted, 2)
                nc.tensor.matmul(bank[0][0:H + 1, 0:P], ones[:, 0:H + 1], diag[:, :], start=True, stop=True
                                 ).then_inc(turned, 1)

            @block.vector
            def _(dve):
                c = Chain(dve, chain)
                c.link(nc.vector.memset(mc[:, :], 0.0))
                nc.vector.tensor_copy(lastf[:, :], srcf[:, T - 1:T]).then_inc(wanted, 1)
                if tag == "init":
                    c.link(nc.vector.tensor_single_scalar(logm[:, :], logm[:, :], 1.0, ALU.max))
                    nc.vector.tensor_copy(count[1][:, :], bank[6][:, 0:NB]).then_inc(dst_done, 1)
                    for h in range(2):
                        c.link(nc.vector.memset(ce[h][:, :, 0], 0.0))
                    dve.wait_ge(dst_done, 5)
                    tot, incl, tmp, mask = (x2[:, o * NB:(o + 1) * NB] for o in range(4))
                    c.link(nc.vector.tensor_copy(tot, bank[1][:, 0:NB]))
                    c.link(nc.vector.tensor_tensor_scan(incl, ones[:, 0:NB], tot, 0.0, ALU.mult, ALU.add))
                    c.link(nc.vector.tensor_tensor(incl, incl, tot, ALU.subtract))
                    c.link(nc.vector.tensor_tensor(tmp, incl, bank[2][:, 0:NB], ALU.add))
                    c.link(nc.vector.tensor_single_scalar(mask, count[1][:, :], 0.0, ALU.is_gt))
                    c.link(nc.vector.tensor_tensor(tmp, tmp, count[1][:, :], ALU.add))
                    c.link(nc.vector.tensor_single_scalar(tmp, tmp, -1.0 - ZROW, ALU.add))
                    c.link(nc.vector.tensor_tensor(tmp, tmp, mask, ALU.mult))
                    c.link(nc.vector.tensor_single_scalar(tmp, tmp, float(ZROW), ALU.add))
                    c.link(nc.vector.tensor_copy(last_i[1][:, :], tmp))
                dve.wait_ge(shifted, 16)
                dve.wait_ge(wanted, 1)
                c.link(nc.vector.tensor_tensor(cont[:, :], srcf[:, 0:1], prevf[:, :], ALU.is_equal))
                c.link(nc.vector.tensor_tensor(fix_f[:, :], lastf[:, :], prevf[:, :], ALU.is_equal))
                nc.vector.tensor_scalar(diag[:, :], ident[:, :], fix_f[:, 0:1], None, ALU.mult).then_inc(wanted, 1)
                dve.wait_ge(wanted, 2)
                junk = sq_all[:, 0:T]
                c.link(nc.vector.tensor_scalar(junk, srcf[:, :], srcf[:, 0:1], None, ALU.is_equal))
                c.link(nc.vector.tensor_reduce(nrun[:, :], junk, AX, ALU.add))
                c.link(nc.vector.tensor_scalar(fix_f[:, :], pidx[:, :], float(T - 1), -1.0 - S, ALU.mult, ALU.add))
                c.link(nc.vector.tensor_tensor(fix_f[:, :], fix_f[:, :], nrun[:, :], ALU.add))
                c.link(nc.vector.tensor_tensor(fix_f[:, :], fix_f[:, :], cont[:, :], ALU.mult))
                c.link(nc.vector.tensor_tensor(fix_f[:, :], fix_f[:, :], pidx[:, :], ALU.add))
                c.link(nc.vector.tensor_single_scalar(fix_f[:, :], fix_f[:, :], float(S), ALU.add))
                c.link(nc.vector.tensor_copy(fix_i[:, :], fix_f[:, :]))
                dve.wait_ge(turned, 1)
                c.link(nc.vector.tensor_copy(chb[:, :], bank[0][0:H + 1, 0:P]))
                c.link(nc.vector.tensor_scalar(penc[:, :], chb[:, :], BIG, -BIG, ALU.mult, ALU.add))

            if tag == "init":
                @block.scalar
                def _(act):
                    act.wait_ge(chain, 2)
                    nc.scalar.activation(logm[:, :], logm[:, :], ACT.Ln)

    GB = 7
    NG = NB // GB
    fin_chain, parts, ps_ok, ex = sem("fin_chain"), sem("parts"), sem("fin_ps"), sem("fin_exp")
    fixed, fix_sent = sem("fix_got"), sem("fix_sent")
    ns_got = [sem(f"ns_got{g}") for g in range(NG)]
    FIN = 12
    fin_before_exp = 9

    def fin_pool(run, key):
        nc.gpsimd.indirect_dma_start(
            out=fx[:, :], out_offset=None, in_=state,
            in_offset=bass.IndirectOffsetOnAxis(ap=fix_i[:, 0:1], axis=0)).then_inc(fixed, 16)
        nc.gpsimd.wait_ge(parts, 4 * run + 4)
        nc.gpsimd.sem_inc(go, 1)
        nc.gpsimd.indirect_dma_start(
            out=state, out_offset=bass.IndirectOffsetOnAxis(ap=fix_i[:, 0:1], axis=0),
            in_=fx[:, :], in_offset=None).then_inc(fix_sent, 16)
        nc.gpsimd.wait_ge(fix_sent, 16 * run + 16)
        nc.gpsimd.sem_inc(go, 1)
        for j in range(NB):
            nc.gpsimd.indirect_dma_start(
                out=ns[:, j, :], out_offset=None, in_=state,
                in_offset=bass.IndirectOffsetOnAxis(ap=last_i[key][:, j:j + 1], axis=0)
            ).then_inc(ns_got[j // GB], 16)

    def fin_pe(pe, run):
        pe.wait_ge(parts, 4 * run + 1)
        nc.tensor.sem_inc(pe_go, 1)
        nc.tensor.transpose(bank[0][0:H + 1, 0:P], vc[:, :], ident[:, :])
        nc.tensor.matmul(bank[1][0:H + 1, 0:P], ones[:, 0:H + 1], diag[:, :], start=True, stop=True
                         ).then_inc(ps_ok, 1)
        pe.wait_ge(parts, 4 * run + 3)
        nc.tensor.sem_inc(pe_go, 1)
        nc.tensor.transpose(bank[2][:, 0:H + 1], vcar[:, 0:P], ident[0:H + 1, 0:H + 1])
        nc.tensor.transpose(bank[3][:, 0:H + 1], mcar[:, 0:P], ident[0:H + 1, 0:H + 1]).then_inc(ps_ok, 1)

    def fin_act(act, run):
        act.wait_ge(parts, 4 * run + 2)
        nc.scalar.activation(arg[:, :], arg[:, :], ACT.Exp).then_inc(ex, 1)
        act.wait_ge(fin_chain, FIN * run + fin_before_exp)
        nc.scalar.activation(fa[:, :], fa[:, :], ACT.Exp).then_inc(ex, 1)

    def fin_dve(dve, run):
        c = Chain(dve, fin_chain, FIN * run)
        nc.vector.tensor_scalar(diag[:, :], ident[:, :], mc[:, 0:1], None, ALU.mult).then_inc(parts, 1)
        c.link(nc.vector.memset(mcar[:, 0:1], -BIG))
        c.link(nc.vector.memset(vcar[:, 0:1], 0.0))
        dve.wait_ge(ps_ok, 2 * run + 1)
        c.link(nc.vector.tensor_copy(mr[:, :], bank[1][0:H + 1, 0:P]))
        c.link(nc.vector.tensor_tensor_scan(mcar[:, 1:P + 1], penc[:, :], mr[:, :], -BIG, ALU.add, ALU.max))
        c.link(nc.vector.tensor_tensor(arg[:, 0:P], mr[:, :], mcar[:, 1:P + 1], ALU.subtract))
        c.link(nc.vector.tensor_tensor(arg[:, P:2 * P], mcar[:, 0:P], mcar[:, 1:P + 1], ALU.subtract))
        nc.vector.scalar_tensor_tensor(arg[:, P:2 * P], arg[:, P:2 * P], 0.0, penc[:, :], ALU.min, ALU.add
                                       ).then_inc(parts, 1)
        dve.wait_ge(ex, 2 * run + 1)
        c.link(nc.vector.tensor_tensor(mr[:, :], arg[:, 0:P], bank[0][0:H + 1, 0:P], ALU.mult))
        nc.vector.tensor_tensor_scan(vcar[:, 1:P + 1], arg[:, P:2 * P], mr[:, :], 0.0, ALU.mult, ALU.add
                                     ).then_inc(parts, 1)
        dve.wait_ge(ps_ok, 2 * run + 2)
        dve.wait_ge(fixed, 16 * run + 16)
        c.link(nc.vector.tensor_tensor(fm[:, :], fx[:, H + 1:ST], bank[3][:, 0:1], ALU.max))
        nc.vector.tensor_tensor(fa[:, 0:1], fx[:, H + 1:ST], fm[:, :], ALU.subtract)
        c.link(nc.vector.tensor_tensor(fa[:, 1:2], bank[3][:, 0:1], fm[:, :], ALU.subtract))
        dve.wait_ge(ex, 2 * run + 2)
        c.link(nc.vector.tensor_tensor(fa[:, 1:2], fa[:, 1:2], cont[:, :], ALU.mult))
        c.link(nc.vector.tensor_scalar(fx[:, 0:H + 1], fx[:, 0:H + 1], fa[:, 0:1], None, ALU.mult))
        c.link(nc.vector.scalar_tensor_tensor(fx[:, 0:H + 1], bank[2][:, 0:H + 1], fa[:, 1:2],
                                              fx[:, 0:H + 1], ALU.mult, ALU.add))
        nc.vector.tensor_copy(fx[:, H + 1:ST], fm[:, :]).then_inc(parts, 1)
        dve.wait_ge(parts, 4 * run + 4)
        c.last(FIN)

    T_SEMS = ("agg_ok", "t1", "t1_sb", "z_ok", "var_h", "std_h", "h_ok", "t2", "t2_sb", "qk_ps", "sq_ok",
              "var_q", "std_q", "row_ok")
    ts = {n: sem(n) for n in T_SEMS}
    turn_chain = {k: sem(f"turn_chain_{k}") for k in ("init", "layer", "last")}
    w_dma, wq_dma, w_ok, w_sb = sem("w_dma"), sem("wq_dma"), sem("w_ok"), sem("w_sb")
    node_dma, q_dma, x_dma = sem("node_dma"), sem("q_dma"), sem("x_dma")
    fill_sent, qc_got = sem("fill_sent"), sem("qc_got")
    deg_root = root_site("deg")
    rows144 = arena[:, 0:NB * 3 * H].rearrange("p (n f) -> p n f", f=3 * H)
    xn = arena[:, 0:NB * H].rearrange("p (n f) -> p n f", f=H)
    sqc = arena[:, NB * 3 * H:NB * 3 * H + GB * 2 * H].rearrange("p (n f) -> p n f", f=H)
    sqb = arena[:, NB * 3 * H + GB * 2 * H:NB * 3 * H + GB * 3 * H].rearrange("p (n f) -> p n f", f=H)
    x1 = hc[:, :, 0:H]
    xd = hc[:, :, OFF:OFF + H]

    def ln_a(c, x, n, sq, st_, var, centred=False):
        if not centred:
            c.link(nc.vector.tensor_reduce(st_, x, AX, ALU.add))
            c.link(nc.vector.tensor_single_scalar(st_, st_, -1.0 / H, ALU.mult))
            c.link(nc.vector.tensor_tensor(x, x, st_.unsqueeze(2).broadcast_to([P, n, H]), ALU.add))
            c.link(nc.vector.tensor_tensor(sq, x, x, ALU.mult))
        c.link(nc.vector.tensor_reduce(st_, sq, AX, ALU.add))
        nc.vector.tensor_scalar(st_, st_, 1.0 / H, 1e-5, ALU.mult, ALU.add).then_inc(var, 1)

    def ln_b(c, x, n, st_, std, at, out):
        c.eng.wait_ge(std, at)
        c.link(nc.vector.reciprocal(st_, st_))
        c.link(nc.vector.tensor_tensor(out, x, st_.unsqueeze(2).broadcast_to([P, n, H]), ALU.mult))

    stb = [sb(f"stb{k}", [P, GB]) for k in range(2)]
    stc = [sb(f"stc{k}", [P, 2 * GB]) for k in range(2)]
    gbo = sb("gbo", [P, 2, H])
    wmean = sb("wmean", [H, 2])

    def turnover(kind, l):
        has_z, has_qk = kind != "init", kind != "last"
        run = 0 if kind == "init" else l + 1
        rz = l
        rq = 0 if kind == "init" else l + 1
        ck = {"init": 0, "layer": l, "last": 0}[kind]
        per = {"init": NG * 17 + 5, "layer": NG * 18 + 5, "last": NG * 22 + 4}[kind]

        def at(r, g):
            return r * NG + g + 1

        with ExitStack() as ctx:
            block = ctx.enter_context(nc.Block(no_gpsimd_drain=True))

            @block.sync
            def _(sp):
                if has_z:
                    sp.dma_start(wmT[:, :], a["wmT"][bass.ds(l, 1), :, :].rearrange("o k f -> (o k) f")
                                 ).then_inc(w_dma, 16)
                    wu_l = a["wu"][bass.ds(l, 1), :, :].rearrange("o k f -> (o k) f")
                    sp.dma_start(wu[0:H, :], wu_l[0:H, :]).then_inc(w_dma, 16)
                    sp.dma_start(wub[:, :], wu_l[H:2 * H, :]).then_inc(w_dma, 16)
                    sp.dma_start(gbo[:, :, :], a["scales"][bass.ds(l, 1), 4:6, :].broadcast_to([P, 2, H])
                                 ).then_inc(w_dma, 16)
                if has_qk:
                    sp.dma_start(wqk[:, :], a["wqk"][bass.ds(rq, 1), :, :].rearrange("o k f -> (o k) f")
                                 ).then_inc(wq_dma, 16)
                    sp.dma_start(gb[:, 0:4, :], a["scales"][bass.ds(rq, 1), 0:4, :].broadcast_to([P, 4, H])
                                 ).then_inc(wq_dma, 16)
                    node_v = nodes.rearrange("(n p) f -> p n f", p=P)
                    q_v = qnodes.rearrange("(n p) f -> p n f", p=P)
                    for g in range(NG):
                        b = slice(g * GB, (g + 1) * GB)
                        sp.wait_ge(ts["row_ok"], at(rq, g))
                        sp.dma_start(node_v[:, b, :], rows144[:, b, H:3 * H]).then_inc(node_dma, 16)
                        sp.dma_start(q_v[:, b, :], rows144[:, b, 0:H]).then_inc(q_dma, 16)
                    sp.wait_ge(node_dma, 16 * NG * (rq + 1))
                    nc.sync.sem_inc(go, 1)
                else:
                    sp.dma_start(xn, a["x_nodes"]).then_inc(x_dma, 16)
                    q_v = qnodes.rearrange("(n p) f -> p n f", p=P)
                    for g in range(NG):
                        b = slice(g * GB, (g + 1) * GB)
                        sp.wait_ge(ts["row_ok"], at(L, g))
                        sp.dma_start(q_v[:, b, :], xd[:, b, :]).then_inc(node_dma, 16)
                    sp.wait_ge(node_dma, 16 * NG * (L + 1))
                    nc.sync.sem_inc(go, 1)

            @block.gpsimd
            def _(pool):
                fin_pool(run, 0)
                if has_qk:
                    for g in range(NG):
                        pool.wait_ge(ts["row_ok"], at(rq, g))
                        nc.gpsimd.sem_inc(go, 1)
                        for j in range(g * GB, (g + 1) * GB):
                            nc.gpsimd.indirect_dma_start(
                                out=fill, out_offset=bass.IndirectOffsetOnAxis(ap=first_i[:, j:j + 1], axis=0),
                                in_=rows144[:, j, 0:H], in_offset=None).then_inc(fill_sent, 16)
                    pool.wait_ge(q_dma, 16 * NG * (rq + 1))
                    nc.gpsimd.sem_inc(go, 1)
                    nc.gpsimd.indirect_dma_start(
                        out=qc[:, :], out_offset=None, in_=qnodes,
                        in_offset=bass.IndirectOffsetOnAxis(ap=first_key[:, 0:1], axis=0)).then_inc(qc_got, 16)
                    pool.wait_ge(fill_sent, 16 * NB * (rq + 1))
                    nc.gpsimd.sem_inc(go, 1)
                    pool.wait_ge(qc_got, 16 * (rq + 1))
                    nc.gpsimd.sem_inc(go, 1)

            @block.tensor
            def _(pe):
                def hold():
                    nc.tensor.sem_inc(pe_go, 1)

                fin_pe(pe, run)
                if has_z:
                    pe.wait_ge(w_dma, 64 * l + 64)
                    hold()
                    nc.tensor.matmul(bank[7][OFF:OFF + H, 0:H], wmT[:, :], wub[:, :], start=True, stop=True
                                     ).then_inc(w_ok, 1)

                def update(g):
                    pe.wait_ge(ts["agg_ok"], at(rz, g))
                    if g == 0:
                        pe.wait_ge(parts, 4 * run + 4)
                    hold()
                    for j in range(GB):
                        ins = nc.tensor.transpose(bank[j // 4][0:HC, (j % 4) * P:(j % 4 + 1) * P],
                                                  hc[:, g * GB + j, 0:HC], ident[:, :])
                    ins.then_inc(ts["t1"], 1)
                    pe.wait_ge(ts["t1_sb"], at(rz, g))
                    if g:
                        pe.wait_ge(ts["var_h"], at(run, g - 1))
                    hold()
                    for j in range(GB):
                        ins = nc.tensor.matmul(bank[2][:, j * H:(j + 1) * H], ht1[0:HC, j * P:(j + 1) * P], wu[:, :],
                                               start=True, stop=True)
                    ins.then_inc(ts["z_ok"], 1)

                def queries(g):
                    pe.wait_ge(ts["h_ok"], at(rq, g))
                    if g == 0:
                        pe.wait_ge(parts, 4 * run + 4)
                    hold()
                    for j in range(GB):
                        ins = nc.tensor.transpose(bank[3 + j // 4][0:H, (j % 4) * P:(j % 4 + 1) * P],
                                                  hc[:, g * GB + j, 0:H], ident[:, :])
                    ins.then_inc(ts["t2"], 1)
                    pe.wait_ge(ts["t2_sb"], at(rq, g))
                    if g:
                        pe.wait_ge(ts["sq_ok"], at(rq, g - 1))
                    hold()
                    for j in range(GB):
                        ins = nc.tensor.matmul(bank[5 + j // 4][:, (j % 4) * 2 * H:(j % 4 + 1) * 2 * H],
                                               ht2[0:H, j * P:(j + 1) * P], wqk[:, :], start=True, stop=True)
                    ins.then_inc(ts["qk_ps"], 1)

                for g in range(-1, NG):
                    if has_z and g + 1 < NG:
                        update(g + 1)
                    if has_qk and g >= 0:
                        queries(g)

            @block.scalar
            def _(act):
                fin_act(act, run)
                if has_z:
                    act.wait_ge(w_ok, l + 1)
                    nc.scalar.copy(wu[OFF:OFF + H, :], bank[7][OFF:OFF + H, 0:H]).then_inc(w_sb, 1)

                def root(var, std, st_, a_):
                    act.wait_ge(ts[var], a_)
                    nc.scalar.activation(st_[:, :], st_[:, :], ACT.Sqrt).then_inc(ts[std], 1)

                def out_of(out, banks, rows):
                    nc.scalar.copy(out[0:rows, 0:4 * P], bank[banks][0:rows, :])
                    return nc.scalar.copy(out[0:rows, 4 * P:GB * P], bank[banks + 1][0:rows, 0:(GB - 4) * P])

                def products(g):
                    act.wait_ge(ts["t2"], at(rq, g))
                    out_of(ht2, 3, H).then_inc(ts["t2_sb"], 1)
                    nc.scalar.copy(rows144[:, g * GB:(g + 1) * GB, 2 * H:3 * H], hc[:, g * GB:(g + 1) * GB, 0:H])
                    act.wait_ge(ts["qk_ps"], at(rq, g))
                    for k, (j0, j1) in enumerate(((0, 4), (4, GB))):
                        src = bank[5 + k][:, 0:(j1 - j0) * 2 * H].rearrange("p (n f) -> p n f", f=2 * H)
                        nc.scalar.activation(flat(sqc[:, 2 * j0:2 * j1, :]), bank[5 + k][:, 0:(j1 - j0) * 2 * H],
                                             ACT.Square)
                        ins = nc.scalar.copy(rows144[:, g * GB + j0:g * GB + j1, 0:2 * H], src)
                    ins.then_inc(ts["sq_ok"], 1)

                if kind == "last":
                    act.wait_ge(deg_root[0], 1)
                    nc.scalar.activation(dis[:, :], dis[:, :], ACT.Sqrt).then_inc(deg_root[1], 1)
                def weighted(g):
                    act.wait_ge(ts["t1"], at(rz, g))
                    if g == 0:
                        act.wait_ge(w_sb, l + 1)
                    out_of(ht1, 0, HC).then_inc(ts["t1_sb"], 1)

                if has_z:
                    weighted(0)
                for g in range(NG + 1):
                    if g < NG:
                        root("var_h", "std_h", stb[g % 2], at(run, g))
                    if g >= 1:
                        if has_qk:
                            root("var_q", "std_q", stc[(g - 1) % 2], at(rq, g - 1))
                        else:
                            act.wait_ge(ts["var_q"], at(L, g - 1))
                            nc.scalar.activation(stc[(g - 1) % 2][:, 0:GB], stc[(g - 1) % 2][:, 0:GB], ACT.Sqrt
                                                 ).then_inc(ts["std_q"], 1)
                    if has_z and g + 1 < NG:
                        weighted(g + 1)
                    if g < NG and has_qk:
                        products(g)

            @block.vector
            def _(dve):
                fin_dve(dve, run)
                c = Chain(dve, turn_chain[kind], per * ck)
                if has_qk:
                    dve.wait_ge(wq_dma, 32 * rq + 32)
                    w3 = wqk[:, :].rearrange("p (o f) -> p o f", o=2)
                    c.link(nc.vector.tensor_reduce(wmean[:, :], w3, AX, ALU.add))
                    c.link(nc.vector.tensor_single_scalar(wmean[:, :], wmean[:, :], -1.0 / H, ALU.mult))
                    c.link(nc.vector.tensor_tensor(w3, w3, wmean[:, :].unsqueeze(2).broadcast_to([H, 2, H]), ALU.add))
                    c.link(nc.vector.memset(mc[:, :], -BIG))
                    c.link(nc.vector.memset(vc[:, :], 0.0))
                else:
                    c.link(nc.vector.memset(vc[:, :], 0.0))
                    nc.vector.tensor_single_scalar(dis[:, :], count[0][:, :], 1.0, ALU.add).then_inc(deg_root[0], 1)
                    dve.wait_ge(deg_root[1], 1)
                    c.link(nc.vector.reciprocal(dis[:, :], dis[:, :]))
                    for h in range(2):
                        nc.vector.memset(so[h][:, :, H:ST], 0.0)
                    c.link(nc.vector.memset(mc[:, :], 0.0))
                    c.link(nc.vector.memset(kc[:, :], -1.0))
                    dve.wait_ge(x_dma, 16)
                if has_z:
                    dve.wait_ge(w_dma, 64 * l + 64)
                inv = stat[:, NB:2 * NB]

                def blocks(t, g):
                    return t[:, g * GB:(g + 1) * GB, :]

                def aggregate(g):
                    dve.wait_ge(ns_got[g], 16 * GB * (run + 1))
                    iv = inv[:, g * GB:(g + 1) * GB]
                    wsum = ns[:, g * GB:(g + 1) * GB, H]
                    if kind == "init":
                        c.link(nc.vector.tensor_single_scalar(iv, wsum, 1e-8, ALU.max))
                    else:
                        c.link(nc.vector.tensor_single_scalar(iv, wsum, 1e-10, ALU.add))
                    c.link(nc.vector.reciprocal(iv, iv))
                    out = blocks(ns[:, :, 0:H] if kind == "init" else xd, g)
                    ins = nc.vector.tensor_tensor(out, blocks(ns[:, :, 0:H], g),
                                                  iv.unsqueeze(2).broadcast_to([P, GB, H]), ALU.mult)
                    if has_z:
                        ins.then_inc(ts["agg_ok"], 1)
                    else:
                        c.link(ins)

                def new_h(g):
                    x = blocks(ns[:, :, 0:H], g)
                    hh = blocks(hc[:, :, 0:H], g)
                    if has_z:
                        dve.wait_ge(ts["z_ok"], at(rz, g))
                        z = bank[2][:, 0:GB * H].rearrange("p (n f) -> p n f", f=H)
                        c.link(nc.vector.tensor_single_scalar(x, z, 0.01, ALU.mult))
                        c.link(nc.vector.tensor_tensor(x, x, z, ALU.max))
                    c.link(nc.vector.tensor_tensor(x, x, hh, ALU.add))
                    ln_a(c, x, GB, sqb, stb[g % 2][:, :], ts["var_h"])

                def new_h_end(g):
                    x = blocks(ns[:, :, 0:H], g)
                    hh = blocks(hc[:, :, 0:H], g)
                    gg = gn if kind == "init" else gbo
                    ln_b(c, x, GB, stb[g % 2][:, :], ts["std_h"], at(run, g), x)
                    c.link(nc.vector.tensor_tensor(x, x, gg[:, 0:1, :].broadcast_to([P, GB, H]), ALU.mult))
                    ins = nc.vector.tensor_tensor(hh, x, gg[:, 1:2, :].broadcast_to([P, GB, H]), ALU.add)
                    if has_qk:
                        ins.then_inc(ts["h_ok"], 1)
                    else:
                        c.link(ins)

                def rows(g):
                    if has_qk:
                        dve.wait_ge(ts["sq_ok"], at(rq, g))
                        ln_a(c, None, 2 * GB, sqc, stc[g % 2][:, :], ts["var_q"], centred=True)
                    else:
                        x = blocks(xn, g)
                        c.link(nc.vector.tensor_tensor(x, x, blocks(hc[:, :, 0:H], g), ALU.add))
                        ln_a(c, x, GB, sqb, stc[g % 2][:, 0:GB], ts["var_q"])

                def rows_end(g):
                    if has_qk:
                        st_ = stc[g % 2]
                        dve.wait_ge(ts["std_q"], at(rq, g))
                        c.link(nc.vector.reciprocal(st_[:, :], st_[:, :]))
                        for o in range(2):
                            x = rows144[:, g * GB:(g + 1) * GB, o * H:(o + 1) * H]
                            s_ = st_[:, :].rearrange("p (n o) -> p n o", o=2)[:, :, o]
                            nc.vector.tensor_tensor(x, x, s_.unsqueeze(2).broadcast_to([P, GB, H]), ALU.mult
                                                    ).then_inc(c.sem, 1)
                            c.k += 1
                        dve.wait_ge(c.sem, c.base + c.k)
                        x = blocks(rows144[:, :, 0:2 * H], g)
                        for o in range(2):
                            gg = gb[:, 2 * o:2 * o + 2, :].rearrange("p a f -> p (a f)"
                                                                     ).unsqueeze(1).broadcast_to([P, GB, 2 * H])
                            ins = nc.vector.tensor_tensor(x, x, gg, (ALU.mult, ALU.add)[o])
                            if o == 0:
                                c.link(ins)
                    else:
                        ln_b(c, blocks(xn, g), GB, stc[g % 2][:, 0:GB], ts["std_q"], at(L, g), blocks(x1, g))
                        ins = nc.vector.tensor_tensor(
                            blocks(xd, g), blocks(x1, g),
                            dis[:, g * GB:(g + 1) * GB].unsqueeze(2).broadcast_to([P, GB, H]), ALU.mult)
                    ins.then_inc(ts["row_ok"], 1)

                aggregate(0)
                for g in range(NG):
                    if g + 1 < NG:
                        aggregate(g + 1)
                    new_h(g)
                    if g >= 1:
                        rows(g - 1)
                    new_h_end(g)
                    if g >= 1:
                        rows_end(g - 1)
                rows(NG - 1)
                rows_end(NG - 1)
                c.last(per)

    edge_pass("init", 0)
    crossings("init")
    turnover("init", 0)
    with nc.Fori(0, L - 1) as l:
        edge_pass("layer", l)
        turnover("layer", l)
    edge_pass("layer", L - 1)
    turnover("last", L - 1)

    edge_pass("nbr", 0)
    crossings("nbr")
    end_chain, out_dma = sem("end_chain"), sem("out_dma")
    with ExitStack() as ctx:
        block = ctx.enter_context(nc.Block())
        run = L + 1

        @block.gpsimd
        def _(pool):
            fin_pool(run, 1)

        @block.tensor
        def _(pe):
            fin_pe(pe, run)

        @block.scalar
        def _(act):
            fin_act(act, run)
            for g in range(NG):
                act.wait_ge(ts["var_h"], run * NG + g + 1)
                nc.scalar.activation(stb[g % 2][:, :], stb[g % 2][:, :], ACT.Sqrt).then_inc(ts["std_h"], 1)

        @block.vector
        def _(dve):
            fin_dve(dve, run)
            c = Chain(dve, end_chain)
            b = [slice(g * GB, (g + 1) * GB) for g in range(NG)]

            def first(g):
                x = xn[:, b[g], :]
                dve.wait_ge(ns_got[g], 16 * GB * (run + 1))
                c.link(nc.vector.tensor_tensor(x, ns[:, b[g], 0:H], xd[:, b[g], :], ALU.add))
                c.link(nc.vector.tensor_tensor(x, x, dis[:, b[g]].unsqueeze(2).broadcast_to([P, GB, H]), ALU.mult))
                c.link(nc.vector.tensor_tensor(x, x, x1[:, b[g], :], ALU.add))
                ln_a(c, x, GB, sqb, stb[g % 2][:, :], ts["var_h"])

            def second(g):
                x = xn[:, b[g], :]
                dve.wait_ge(ts["std_h"], run * NG + g + 1)
                c.link(nc.vector.reciprocal(stb[g % 2][:, :], stb[g % 2][:, :]))
                nc.vector.tensor_tensor(x, x, stb[g % 2][:, :].unsqueeze(2).broadcast_to([P, GB, H]), ALU.mult
                                        ).then_inc(ts["row_ok"], 1)

            first(0)
            for g in range(1, NG):
                first(g)
                second(g - 1)
            second(NG - 1)

        @block.sync
        def _(sp):
            full = N // P
            for g in range(NG):
                sp.wait_ge(ts["row_ok"], run * NG + g + 1)
                n0, n1 = g * GB, min((g + 1) * GB, full)
                sp.dma_start(a["out"][n0 * P:n1 * P, :].rearrange("(n p) f -> p n f", p=P), xn[:, n0:n1, :]
                             ).then_inc(out_dma, 16)
            sp.dma_start(a["out"][full * P:N, :], xn[0:N - full * P, full, :]).then_inc(out_dma, 16)
            sp.wait_ge(out_dma, 16 * (NG + 1))



def kernel(**inputs):
    import numpy as np
    import concourse.bacc as bacc
    from concourse.bass_utils import run_bass_kernel_spmd as run

    def pad(x, n, value):
        x = np.asarray(x)
        return np.concatenate([x, np.full((n - x.shape[0],) + x.shape[1:], value, x.dtype)], axis=0)

    def node_cols(x, value):
        x = pad(x, NN, value).reshape((NB, P) + np.asarray(x).shape[1:])
        return np.ascontiguousarray(np.moveaxis(x, 0, 1))

    w = {k[7:]: np.ascontiguousarray(v) for k, v in inputs.items() if k.startswith("L0_gnn_")}
    arrays = {
        "edge_attr": pad(inputs["edge_attr_40"], S, 0),
        "edge_weight": pad(inputs["edge_weight"], S, 0).reshape(P, T),
        "x_nodes": node_cols(inputs["x"], 0),
        "mult_nodes": node_cols(inputs["node_vec"], 1),
        "type_nodes": node_cols(inputs["node_type_119"], 0),
        "wqk": np.ascontiguousarray(np.concatenate([w["Wq"], w["Wk"]], axis=2)),
        "wmT": np.ascontiguousarray(w["Wm"].transpose(0, 2, 1)),
        "wu": w["Wu"],
        "scales": np.ascontiguousarray(np.stack([w[k] for k in ("gq", "gk", "bq", "bk", "go", "bo")], axis=1)),
        "gnbn": np.ascontiguousarray(np.stack([w["gn"], w["bn"]])),
        "f1w": w["F1W"],
        "f1b": w["F1b"].reshape(H, 1),
        "f2": np.ascontiguousarray(np.concatenate([w["F2W"], w["F2b"][None, :]], axis=0)),
        "emb": w["emb"],
        "adapt": w["adapt"],
    }
    for name in ("src", "dst"):
        cols = pad(inputs[name], S, N).reshape(P, T)
        arrays[f"{name}_cols"] = cols
        arrays[f"{name}_rows"] = np.ascontiguousarray(cols.T).reshape(1, S)
    nc = bacc.Bacc("TRN2", target_bir_lowering=False, num_devices=1)
    aps = {k: nc.dram_tensor(f"in_{k}", v.shape, mybir.dt.from_np(v.dtype), kind="ExternalInput").ap()
           for k, v in arrays.items()}
    aps["out"] = nc.dram_tensor("out_0", (N, H), F32, kind="ExternalOutput").ap()
    build(nc, aps)
    r = run(nc, [{f"in_{k}": v for k, v in arrays.items()}], core_ids=[0])
    return r.results[0]["out_0"]
```
